# Optimizing a Trainium2 kernel written in Bass

```python
import numpy as np
import jax
import jax.numpy as jnp

def _softmax(x, axis=-1):
    return jax.nn.softmax(x, axis=axis)
def _gelu(x):
    return jax.nn.gelu(x, approximate=True)
def _silu(x):
    return jax.nn.silu(x)
def _sigmoid(x):
    return jax.nn.sigmoid(x)
def _layernorm(x, axis=-1, eps=1e-5):
    m = jnp.mean(x, axis=axis, keepdims=True)
    v = jnp.var(x, axis=axis, keepdims=True)
    return (x - m) / jnp.sqrt(v + eps)
def _scatter_add(tgt, idx, src, axis=0):
    return tgt.at[idx].add(src)
def _segment_sum(src, seg, n):
    return jax.ops.segment_sum(src, seg, n)

kernel_name = 'mk_conv_preact_d1_conv_nchw192_9b1ea6'

def setup_inputs(seed: int = 0):
    np.random.seed(seed)
    _w = jnp.asarray
    def _rec_inputs():
        import jax
        import jax.numpy as jnp
        _gk = jax.random.key(seed)
        x = -0.0002221 + 1 * jax.random.normal(jax.random.fold_in(_gk, 1), (2, 192, 256, 256), jnp.float32)
        return x
    x = _rec_inputs()
    def _L0_conv_setup():
        import jax, jax.numpy as jnp
        import numpy as np
        DIM = 192
        HEADS = 8
        EPS = 1e-12

        def _l2norm(t):
            n = jnp.sqrt(jnp.sum(t * t, axis=-1, keepdims=True))
            return t / jnp.maximum(n, EPS)
        key = jax.random.key(seed)
        k1, k2, k3, k4 = jax.random.split(key, 4)
        b, c, h, w = (2, DIM, 256, 256)
        x = jax.random.normal(k1, (b, c, h, w), dtype=jnp.float32)
        qkv_w = jax.random.normal(k2, (3 * c, c), dtype=jnp.float32) * (1.0 / np.sqrt(c))
        dw_w = jax.random.normal(k3, (3 * c, 1, 3, 3), dtype=jnp.float32) * (1.0 / 3.0)
        proj_w = jax.random.normal(k4, (c, c), dtype=jnp.float32) * (1.0 / np.sqrt(c))
        temperature = jnp.ones((HEADS, 1, 1), dtype=jnp.float32)
        return {'x': x, 'qkv_w': qkv_w, 'dw_w': dw_w, 'proj_w': proj_w, 'temperature': temperature}
    _L0_conv_all = _L0_conv_setup()
    _L0_conv_in = {k: v for k, v in _L0_conv_all.items() if k in ('qkv_w', 'dw_w', 'proj_w', 'temperature', )}
    del _L0_conv_all

    return {
        "x": x,
        "L0_conv_qkv_w": _L0_conv_in["qkv_w"],
        "L0_conv_dw_w": _L0_conv_in["dw_w"],
        "L0_conv_proj_w": _L0_conv_in["proj_w"],
        "L0_conv_temperature": _L0_conv_in["temperature"],
    }

def reference(x, L0_conv_qkv_w, L0_conv_dw_w, L0_conv_proj_w, L0_conv_temperature):
    import jax
    import jax.numpy as jnp
    def _L0_conv_ref(x, qkv_w, dw_w, proj_w, temperature):
        import jax, jax.numpy as jnp
        import numpy as np
        DIM = 192
        HEADS = 8
        EPS = 1e-12

        def _l2norm(t):
            n = jnp.sqrt(jnp.sum(t * t, axis=-1, keepdims=True))
            return t / jnp.maximum(n, EPS)
        b, c, h, w = x.shape
        qkv = jnp.einsum('oc,bchw->bohw', qkv_w, x)
        qkv = jax.lax.conv_general_dilated(qkv, dw_w, window_strides=(1, 1), padding='SAME', feature_group_count=3 * c, dimension_numbers=('NCHW', 'OIHW', 'NCHW'))
        q, k, v = jnp.split(qkv, 3, axis=1)
        q = q.reshape(b, HEADS, c, -1)
        k = k.reshape(b, HEADS, c, -1)
        v = v.reshape(b, HEADS, c, -1)
        q = _l2norm(q)
        k = _l2norm(k)
        attn = jnp.einsum('bhcn,bhdn->bhcd', q, k) * temperature
        attn = jax.nn.softmax(attn, axis=-1)
        out = jnp.einsum('bhcd,bhdn->bhcn', attn, v)
        out = out.reshape(b, c, h, w)
        out = jnp.einsum('oc,bchw->bohw', proj_w, out)
        return out

    def _gn(v, G=32, eps=1e-5):
        B_, C_, H_, W_ = v.shape
        g = v.reshape(B_, G, C_ // G, H_, W_)
        m = jnp.mean(g, axis=(2, 3, 4), keepdims=True)
        s = jnp.var(g, axis=(2, 3, 4), keepdims=True)
        return ((g - m) / jnp.sqrt(s + eps)).reshape(v.shape)

    def _ln_c(v, eps=1e-6):
        m = jnp.mean(v, axis=1, keepdims=True)
        s = jnp.var(v, axis=1, keepdims=True)
        return (v - m) / jnp.sqrt(s + eps)

    def _ln_t(v, eps=1e-5):
        m = jnp.mean(v, axis=-1, keepdims=True)
        s = jnp.var(v, axis=-1, keepdims=True)
        return (v - m) / jnp.sqrt(s + eps)

    def _to_tokens(v):
        B_, C_, H_, W_ = v.shape
        return v.reshape(B_, C_, H_ * W_).transpose(0, 2, 1)
    def _from_tokens(t, like):
        B_, C_, H_, W_ = like.shape
        return t.transpose(0, 2, 1).reshape(B_, C_, H_, W_)

    x = x + _L0_conv_ref(_gn(x), L0_conv_qkv_w, L0_conv_dw_w, L0_conv_proj_w, L0_conv_temperature)
    return x


_drawn_inputs = setup_inputs


def setup_inputs(seed=0):
    import zlib

    import numpy as np

    out = dict(_drawn_inputs(seed))
    spreads = {'L0_conv_temperature': (1.0, 0.2)}
    factors = {}
    for name, (base, spread) in spreads.items():
        noise = np.random.default_rng([zlib.crc32(name.encode()), seed]).standard_normal(out[name].shape)
        drawn = base * np.exp(spread * noise) if base else spread * noise
        out[name] = jnp.asarray(drawn.astype(out[name].dtype))
    for name, factor in factors.items():
        out[name] = (out[name] * factor).astype(out[name].dtype)
    return out
```

```python
from contextlib import ExitStack

import concourse.bass as bass
from concourse import mybir

ALU = mybir.AluOpType
ACT = mybir.ActivationFunctionType
F32 = mybir.dt.float32
BF16 = mybir.dt.bfloat16
AX_X = mybir.AxisListType.X

P = 128
BATCH, C, H, W = 2, 192, 256, 256
HEADS, HC = 8, 24
CHUNKS = 8
RPC = H // CHUNKS
HALF = CHUNKS // 2
REST = C - P
L = HC * CHUNKS
LP = L // 2
SETS, STEPS = RPC + 2, RPC
PAD = W + 2
GROUPS = 32
GN_EPS, NORM_EPS = 1e-5, 1e-12
GN_CHUNK = 4096
GN_CHUNKS = C * H * W // P // GN_CHUNK
BN = 512
TAPS = [(dy, dx) for dy in range(3) for dx in range(3)]
BANK = 512
DMA = 16
CONSTS = 12


def conv_preact_kernel(nc, x, w_qkv_t, dw, proj_t, temperature, ident_in, group_avg_in, group_sel_in, out):
    inv_norms = nc.dram_tensor("inv_norms", [2 * C, CHUNKS], F32).ap()
    v_rows = nc.dram_tensor("v_rows", [2, C, CHUNKS, W], F32).ap()

    x_sets = x.rearrange("b c (s r) w -> b c s r w", s=CHUNKS)
    out_sets = out.rearrange("b c (s r) w -> b c s r w", s=CHUNKS)
    x_flat = x.rearrange("b c h w -> b (c h w)").rearrange("b (p k n) -> b p k n", p=P, n=GN_CHUNK)

    with ExitStack() as ctx:
        nc.disable_value_cache = True
        ctx.enter_context(nc.allow_non_contiguous_dma("norms of a few KB are permuted"))

        def sb(name, shape, dt=F32):
            return ctx.enter_context(nc.sbuf_tensor(name, shape, dt))

        def sem(name):
            return ctx.enter_context(nc.semaphore(name))

        w_main = sb("w_main", [P, 3 * C])
        w_rest = sb("w_rest", [P, 3 * C])
        taps = sb("taps", [P, 5, 9])
        proj_main = sb("proj_main", [P, C])
        proj_rest_mem = sb("proj_rest", [P, C])
        proj_rest = proj_rest_mem[REST:P, :]
        ident = sb("ident", [P, P])
        group_avg = sb("group_avg", [P, P])
        group_sel = sb("group_sel", [P, 2, P])
        temp = sb("temp", [LP, HEADS])
        zeros = sb("zeros", [P, W])
        gn = sb("gn", [P, 16])
        gn_scale = sb("gn_scale", [P, 2])
        gn_bias = sb("gn_bias", [P, 2])
        sumsq = sb("sumsq", [P, 3, CHUNKS])
        sq_step = sb("sq_step", [P, 2, 3, CHUNKS])
        nrm = sb("nrm", [P, 4, 3, CHUNKS])
        row_scale = sb("row_scale", [LP, HEADS, 2])
        soft = sb("soft", [LP, 4, HEADS, 2])
        attn_t = sb("attn_t", [LP, 2, HEADS, L])
        x_ring = sb("x_ring", [P, 2, 12, W])
        scores_mem = sb("scores_mem", [P, HEADS * 2 * L])
        u_mem = sb("u_mem", [P, 4 * 3 * CHUNKS * PAD])
        conv_mem = sb("conv_mem", [P, 2 * CHUNKS * W])
        qk_mem = sb("qk_mem", [P, CHUNKS * 2 * 2 * C])
        junk = sb("junk", [P, CHUNKS, W], BF16)

        gn_in = [conv_mem[:, :], qk_mem[:, 0:GN_CHUNK]]
        bn = qk_mem[:, GN_CHUNK:GN_CHUNK + GN_CHUNKS * (GN_CHUNK // BN) * 6].rearrange("p (k s) -> p k s", s=6)
        scores = scores_mem[0:LP, :].rearrange("p (h n) -> p h n", h=HEADS)
        u1 = u_mem[:, :].rearrange("p (m q s w) -> p m q s w", m=3, q=4, s=CHUNKS)
        conv1 = conv_mem[:, :].rearrange("p (q s w) -> p q s w", q=2, s=CHUNKS)
        qk_t = qk_mem[:, :].rearrange("p (x c s) -> p x c s", x=2, s=CHUNKS)
        logits = qk_mem[0:LP, 0:HEADS * 2 * L].rearrange("p (h g n) -> p h g n", h=HEADS, g=2)
        k_scale = conv_mem[0:LP, 0:HEADS * L].rearrange("p (h n) -> p h n", h=HEADS)
        t0, t1 = 4 * CHUNKS * PAD, 6 * CHUNKS * PAD
        u2_main = u1[:, 0]
        u2_rest = u_mem[:, t0:t1].rearrange("p (q s w) -> p q s w", q=4, s=HALF)
        o = t1
        resid = u_mem[:, o:o + 2 * 12 * W].rearrange("p (q s w) -> p q s w", q=2, s=12)
        o += 2 * 12 * W
        ao_main = u_mem[:, o:o + CHUNKS * W].rearrange("p (s w) -> p s w", s=CHUNKS)
        o += CHUNKS * W
        ao_rest = u_mem[REST:P, o:o + CHUNKS * W].rearrange("p (s w) -> p s w", s=CHUNKS)
        o += CHUNKS * W
        assert o <= 12 * CHUNKS * PAD
        v_main = conv1
        v_rest = qk_mem[:, 0:2 * HALF * W].rearrange("p (q s w) -> p q s w", q=2, s=HALF)
        o = 2 * HALF * W
        v_in = qk_mem[0:LP, o:o + 2 * HEADS * W].rearrange("p (h w) -> p h w", h=2 * HEADS)
        o_t = scores_mem[:, :].rearrange("p (x c s) -> p x c s", x=2, s=CHUNKS)

        psum = ctx.enter_context(nc.psum_tensor("psum", [P, 8, BANK], F32))

        consts_loaded = sem("consts_loaded")
        zeroed = sem("zeroed")
        gn_loaded = [sem("gn_loaded0"), sem("gn_loaded1")]
        gn_read = sem("gn_read")
        gn_dve = sem("gn_dve")
        gn_pe = sem("gn_pe")
        gn_act = sem("gn_act")
        gn_step, soft_step = sem("gn_step"), sem("soft_step")
        sums_zeroed = sem("sums_zeroed")
        x1_loaded = [sem("x1_loaded0"), sem("x1_loaded1")]
        x1_normed = sem("x1_normed")
        u1_ready, u1_evac = sem("u1_ready"), sem("u1_evac")
        mac1, conv1_done = sem("mac1"), sem("conv1_done")
        qkt_ready, qkt_evac = sem("qkt_ready"), sem("qkt_evac")
        squared, sq_added = sem("squared"), sem("sq_added")
        scores_ready, scores_added = sem("scores_ready"), sem("scores_added")
        soft_act, soft_dve, soft_pe, soft_dma = sem("soft_act"), sem("soft_dve"), sem("soft_pe"), sem("soft_dma")
        attn_t_evac = sem("attn_t_evac")
        x2_loaded = [sem("x2_loaded0"), sem("x2_loaded1")]
        x2_normed = sem("x2_normed")
        u2_ready, u2_evac = sem("u2_ready"), sem("u2_evac")
        mac2, conv2_done = sem("mac2"), sem("conv2_done")
        v_stored = [sem("v_stored0"), sem("v_stored1")]
        v_loaded = sem("v_loaded")
        ot_ready, ot_evac = sem("ot_ready"), sem("ot_evac")
        ao_ready, ao_evac = sem("ao_ready"), sem("ao_evac")
        proj_ready, resid_done = sem("proj_ready"), sem("resid_done")
        resid_loaded = [sem("resid_loaded0"), sem("resid_loaded1")]
        out_stored = [sem("out_stored0"), sem("out_stored1")]

        block = ctx.enter_context(nc.Block())

        def walk(eng, body):
            for c in range(2, 6):
                body(0, c)
            with eng.Fori(1, STEPS // 4 - 1) as i:
                for c in range(2, 6):
                    body(i, c)
            for c in range(2, 6):
                body(STEPS // 4 - 1, c)

        def first(i, c, t):
            return isinstance(i, int) and 4 * i + c < t

        def at(i, c):
            return 4 * i + c if isinstance(i, int) else None

        def move(i, c, by):
            return i, c + by

        @block.sync
        def _(sp):
            sp.dma_start(w_main[:, :], w_qkv_t[0:P, :]).then_inc(consts_loaded, DMA)
            for half in range(2):
                rows = slice(REST * half, REST * (half + 1))
                sp.dma_start(w_rest[rows, :], w_qkv_t[P:C, :]).then_inc(consts_loaded, DMA)
                sp.dma_start(taps[rows, 4, :], dw[2 * C + P:3 * C, :]).then_inc(consts_loaded, DMA)
            sp.dma_start(taps[:, 0:4, :], dw[0:4 * P, :].rearrange("(m p) k -> p m k", p=P)).then_inc(consts_loaded, DMA)
            sp.dma_start(proj_main[:, :], proj_t[0:P, :]).then_inc(consts_loaded, DMA)
            sp.dma_start(proj_rest, proj_t[P:C, :]).then_inc(consts_loaded, DMA)
            sp.dma_start(ident[:, :], ident_in[:, :]).then_inc(consts_loaded, DMA)
            sp.dma_start(group_avg[:, :], group_avg_in[:, :]).then_inc(consts_loaded, DMA)
            sp.dma_start(group_sel[:, :, :], group_sel_in[:, :, :]).then_inc(consts_loaded, DMA)
            sp.dma_start(temp[:, :], temperature[:, :].partition_broadcast(LP)).then_inc(consts_loaded, DMA)

            def load_set(b, i, c, loaded):
                t, q = at(i, c), c % 2
                sp.wait_ge(consts_loaded, CONSTS * DMA)
                lo, hi = (1 if t == 0 else 0), (CHUNKS - 1 if t == SETS - 1 else CHUNKS)
                if t == 0:
                    row = lambda c0, c1, s0, s1: x_sets[b, c0:c1, s0 - 1:s1 - 1, RPC - 1, :]
                elif t == SETS - 1:
                    row = lambda c0, c1, s0, s1: x_sets[b, c0:c1, s0 + 1:s1 + 1, 0, :]
                else:
                    row = lambda c0, c1, s0, s1: x_sets[b, c0:c1, s0:s1, 4 * i + c - 1, :]
                sp.dma_start(x_ring[:, q, lo:hi, :], row(0, P, lo, hi)).then_inc(loaded[q], DMA)
                sp.dma_start(x_ring[0:REST, q, 8 + lo:12, :], row(P, C, lo, HALF)).then_inc(loaded[q], DMA)
                sp.dma_start(x_ring[REST:P, q, 8:hi + 4, :], row(P, C, HALF, hi)).then_inc(loaded[q], DMA)

            with sp.Fori(0, BATCH) as b:
                def gn_load(k, q):
                    sp.wait_ge(consts_loaded, CONSTS * DMA)
                    sp.dma_start(gn_in[q], x_flat[b, :, k, :]).then_inc(gn_loaded[q], DMA)

                gn_load(0, 0)
                gn_load(1, 1)
                with sp.Fori(1, GN_CHUNKS // 2) as i:
                    for q in range(2):
                        sp.wait_ge(gn_read, b * GN_CHUNKS + 2 * i + q - 1)
                        gn_load(2 * i + q, q)

                load_set(b, 0, 0, x1_loaded)
                load_set(b, 0, 1, x1_loaded)

                def step1(i, c):
                    sp.wait_ge(u1_ready, 6 * (SETS * b + 4 * i + c - 1))
                    load_set(b, i, c, x1_loaded)

                walk(sp, step1)

                sp.wait_ge(soft_dve, 5 * b + 1)
                sp.dma_start(inv_norms.rearrange("(m p) s -> p m s", p=P), nrm[:, 3]).then_inc(soft_dma, DMA)
                sp.wait_ge(soft_dma, DMA * (3 * b + 1))
                q_norms = inv_norms[0:C, :].rearrange("c s -> (c s)").rearrange("(h g p) -> p h g", g=2, p=LP)
                sp.dma_start(row_scale[:, :, :], q_norms).then_inc(soft_dma, DMA)
                k_norms = inv_norms[C:2 * C, :].rearrange("(o c) s -> o (c s)", o=1)
                sp.dma_start(conv_mem[0:LP, 0:HEADS * L], k_norms.partition_broadcast(LP)).then_inc(soft_dma, DMA)

                def load_resid(i, c):
                    q = c % 2
                    r = 4 * i + c - 2
                    sp.wait_ge(consts_loaded, CONSTS * DMA)
                    sp.dma_start(resid[:, q, 0:8, :], x_sets[b, 0:P, :, r, :]).then_inc(resid_loaded[q], DMA)
                    sp.dma_start(resid[0:REST, q, 8:12, :], x_sets[b, P:C, 0:HALF, r, :]).then_inc(resid_loaded[q], DMA)
                    sp.dma_start(resid[REST:P, q, 8:12, :], x_sets[b, P:C, HALF:CHUNKS, r, :]).then_inc(resid_loaded[q], DMA)

                def store_v(i, c):
                    q = c % 2
                    sp.wait_ge(conv2_done, 2 * (STEPS * b + 4 * i + c - 1))
                    sp.dma_start(v_rows[q, 0:P], v_main[:, q]).then_inc(v_stored[q], DMA)
                    sp.dma_start(v_rows[q, P:C, 0:HALF], v_rest[0:REST, q]).then_inc(v_stored[q], DMA)
                    sp.dma_start(v_rows[q, P:C, HALF:CHUNKS], v_rest[REST:P, q]).then_inc(v_stored[q], DMA)

                def load_v(i, c):
                    q = c % 2
                    sp.wait_ge(v_stored[q], 3 * DMA * (STEPS // 2 * b + 2 * i + (c - 2) // 2 + 1))
                    if not first(i, c, 3):
                        sp.wait_ge(ot_ready, 8 * (STEPS * b + 4 * i + c - 2))
                    sp.dma_start(v_in, v_rows[q].rearrange("c s w -> (c s) w").rearrange("(h p) w -> p h w", p=LP)).then_inc(v_loaded, DMA)

                def store_out(i, c):
                    q, r = c % 2, 4 * i + c - 2
                    sp.wait_ge(resid_done, 6 * (STEPS * b + r + 1))
                    sp.wait_ge(consts_loaded, CONSTS * DMA)
                    sp.dma_start(out_sets[b, 0:P, :, r, :], resid[:, q, 0:8, :]).then_inc(out_stored[q], DMA)
                    sp.dma_start(out_sets[b, P:C, 0:HALF, r, :], resid[0:REST, q, 8:12, :]).then_inc(out_stored[q], DMA)
                    sp.dma_start(out_sets[b, P:C, HALF:CHUNKS, r, :], resid[REST:P, q, 8:12, :]).then_inc(out_stored[q], DMA)

                def load_next(i, c):
                    sp.wait_ge(u2_ready, 6 * (SETS * b + 4 * i + c + 1))
                    load_set(b, *move(i, c, 2), x2_loaded)

                load_set(b, 0, 0, x2_loaded)
                load_set(b, 0, 1, x2_loaded)
                load_resid(0, 2)
                load_resid(0, 3)

                for c in (0, 1):
                    load_next(0, c)

                def step2(i, c):
                    if at(i, c) is None or at(i, c) + 2 < SETS:
                        load_next(i, c)
                    if not first(i, c, 3):
                        store_v(*move(i, c, -1))
                        load_v(*move(i, c, -1))
                    if not first(i, c, 5):
                        j, d = move(i, c, -3)
                        store_out(j, d)
                        sp.wait_ge(out_stored[d % 2], 3 * DMA * (STEPS // 2 * b + 2 * j + (d - 2) // 2 + 1))
                        load_resid(j, d + 2)

                walk(sp, step2)
                last = STEPS // 4 - 1
                store_v(last, 5)
                load_v(last, 5)
                store_out(last, 3)
                sp.wait_ge(out_stored[1], 3 * DMA * (STEPS // 2 * b + 2 * last + 1))
                load_resid(last, 5)
                store_out(last, 4)
                store_out(last, 5)

            for q in range(2):
                sp.wait_ge(out_stored[q], 3 * DMA * STEPS // 2 * BATCH)

        @block.tensor
        def _(pe):
            pe.wait_ge(consts_loaded, CONSTS * DMA)

            def x_tile(q, s, n):
                half, l = s // HALF, s % HALF
                rows = slice(REST * half, REST * (half + 1))
                return x_ring[:, q, s:s + n, :], rows, x_ring[rows, q, 8 + l:8 + l + n, :]

            def first_conv1(b, i, c):
                T = SETS * b + 4 * i + c
                pe.wait_ge(x1_normed, T + 1)
                for m in range(3):
                    for half in range(2):
                        g = 2 * m + half
                        if not (first(i, c, 1) and g < 2):
                            pe.wait_ge(u1_evac, 6 * T + g - 1)
                        for j in range(2):
                            x0, rows, x1 = x_tile(c % 2, HALF * half + 2 * j, 2)
                            bank = psum[:, 2 * half + j, :]
                            pe.matmul(bank, w_main[:, P * m:P * (m + 1)], x0, start=True, stop=False)
                            mm = pe.matmul(bank, w_rest[rows, P * m:P * (m + 1)], x1, start=False, stop=True)
                        mm.then_inc(u1_ready, 1)

            def transpose_qk(b, i, c, m):
                n = 3 * (STEPS * b + 4 * i + c - 2) + m
                pe.wait_ge(conv1_done, n + 1)
                for j in range(4):
                    if not (first(i, c, 3) and m == 0 and j < 2):
                        pe.wait_ge(qkt_evac, 4 * n + j - 1)
                    for a in range(4):
                        mm = pe.transpose(psum[:, 4 + j % 2, P * a:P * (a + 1)],
                                          conv1[:, (c + m) % 2, HALF * (j % 2) + a, P * (j // 2):P * (j // 2 + 1)], ident[:, :])
                    mm.then_inc(qkt_ready, 1)

            def head_rows(xh, c0):
                return qk_t[:, xh, c0:c0 + HC, :].rearrange("p j s -> p (j s)")

            def make_scores(b, i, c):
                n = STEPS * b + 4 * i + c - 2
                pe.wait_ge(qkt_evac, 12 * (n + 1))
                for h in range(HEADS):
                    if not (first(i, c, 3) and h < 2):
                        pe.wait_ge(scores_added, 8 * n + h - 1)
                    for g in range(2):
                        for xh in range(2):
                            mm = pe.matmul(psum[0:LP, 6 + h % 2, L * g:L * (g + 1)],
                                           head_rows(xh, HC * h)[:, LP * g:LP * (g + 1)],
                                           head_rows(xh, C + HC * h), start=xh == 0, stop=xh == 1)
                    mm.then_inc(scores_ready, 1)

            def first_conv2(b, i, c):
                T = SETS * b + 4 * i + c
                pe.wait_ge(x2_normed, T + 1)
                for g in range(6):
                    if not (first(i, c, 1) and g < 2):
                        pe.wait_ge(u2_evac, 6 * T + g - 1)
                    if g < 4:
                        x0, rows, x1 = x_tile(c % 2, 2 * g, 2)
                        bank = psum[:, g % 2, :]
                        pe.matmul(bank, w_main[:, 2 * C:2 * C + P], x0, start=True, stop=False)
                        mm = pe.matmul(bank, w_rest[rows, 2 * C:2 * C + P], x1, start=False, stop=True)
                    else:
                        for half in range(2):
                            x0, rows, x1 = x_tile(c % 2, HALF * half + 2 * (g - 4), 2)
                            bank = psum[REST * half:REST * (half + 1), g % 2, :]
                            pe.matmul(bank, w_main[:, 2 * C + P:3 * C], x0, start=True, stop=False)
                            mm = pe.matmul(bank, w_rest[rows, 2 * C + P:3 * C], x1, start=False, stop=True)
                    mm.then_inc(u2_ready, 1)

            def attend(b, i, c):
                n = STEPS * b + 4 * i + c - 2
                pe.wait_ge(v_loaded, DMA * (n + 1))
                for k in range(8):
                    if not (first(i, c, 3) and k < 2):
                        pe.wait_ge(ot_evac, 8 * n + k - 1)
                    xh, h0 = k // 4, 2 * (k % 4)
                    for h in range(h0, h0 + 2):
                        for g in range(2):
                            mm = pe.matmul(psum[:, 2 + k % 2, L * (h - h0):L * (h - h0 + 1)],
                                           v_in[:, 2 * h + g, P * xh:P * (xh + 1)], attn_t[:, g, h, :], start=g == 0, stop=g == 1)
                    mm.then_inc(ot_ready, 1)
                pe.wait_ge(ot_evac, 8 * (n + 1))
                for k in range(8):
                    if not (first(i, c, 3) and k < 2):
                        pe.wait_ge(ao_evac, 8 * n + k - 1)
                    s, c0, c1 = 2 * (k // 2), REST * (k % 2), P + REST * (k % 2)
                    for a in range(4):
                        mm = pe.transpose(psum[:, 4 + k % 2, P * a:P * (a + 1)],
                                          o_t[:, a % 2, c0:c1, s + a // 2], ident[:, :])
                    mm.then_inc(ao_ready, 1)

            def project(b, i, c):
                n = STEPS * b + 4 * i + c - 2
                pe.wait_ge(ao_evac, 8 * (n + 1))
                for g in range(6):
                    if not (first(i, c, 3) and g < 2):
                        pe.wait_ge(resid_done, 6 * n + g - 1)
                    for half in ([0] if g < 4 else [0, 1]):
                        s = 2 * g if g < 4 else HALF * half + 2 * (g - 4)
                        rows, cols = (slice(0, P), slice(0, P)) if g < 4 else (
                            slice(REST * half, REST * (half + 1)), slice(P, C))
                        bank = psum[rows, 6 + g % 2, :]
                        pe.matmul(bank, proj_main[:, cols], ao_main[:, s:s + 2, :], start=True, stop=False)
                        mm = pe.matmul(bank, proj_rest[:, cols], ao_rest[:, s:s + 2, :], start=False, stop=True)
                    mm.then_inc(proj_ready, 1)

            with pe.Fori(0, BATCH) as b:
                pe.wait_ge(gn_dve, 5 * b + 1)
                pe.matmul(psum[:, 0, 0:2], group_avg[:, :], gn[:, 0:2], start=True, stop=True).then_inc(gn_pe, 1)
                pe.wait_ge(gn_dve, 5 * b + 2)
                pe.matmul(psum[:, 1, 0:2], group_sel[:, 0, :], gn[:, 4:6], start=True, stop=True)
                pe.matmul(psum[:, 1, 2:4], group_sel[:, 1, :], gn[:, 4:6], start=True, stop=True).then_inc(gn_pe, 1)

                for c in range(3):
                    first_conv1(b, 0, c)

                def step1(i, c):
                    if at(i, c) != SETS - 1:
                        first_conv1(b, *move(i, c, 1))
                    for m in range(3):
                        transpose_qk(b, i, c, m)
                    make_scores(b, i, c)

                walk(pe, step1)

                pe.wait_ge(soft_dve, 5 * b + 5)
                for k in range(8):
                    g, h0 = k // 4, 2 * (k % 4)
                    if k >= 2:
                        pe.wait_ge(attn_t_evac, 8 * b + k - 1)
                    for h in range(h0, h0 + 2):
                        for gq in range(2):
                            mm = pe.transpose(psum[0:LP, 4 + k % 2, L * (h - h0) + LP * gq:L * (h - h0) + LP * (gq + 1)],
                                              logits[:, h, gq, LP * g:LP * (g + 1)], ident[0:LP, 0:LP])
                    mm.then_inc(soft_pe, 1)
                pe.wait_ge(attn_t_evac, 8 * (b + 1))

                for c in range(3):
                    first_conv2(b, 0, c)

                def step2(i, c):
                    if at(i, c) != SETS - 1:
                        first_conv2(b, *move(i, c, 1))
                    if not first(i, c, 4):
                        project(b, *move(i, c, -2))
                    if not first(i, c, 3):
                        attend(b, *move(i, c, -1))

                walk(pe, step2)
                last = STEPS // 4 - 1
                project(b, last, 4)
                attend(b, last, 5)
                project(b, last, 5)

        @block.scalar
        def _(act):
            act.wait_ge(zeroed, 1)

            def normalise(b, i, c, loaded, normed):
                t, q = at(i, c), c % 2
                act.wait_ge(loaded[q], 3 * DMA * (SETS // 2 * b + 2 * i + c // 2 + 1))
                lo, hi = (1 if t == 0 else 0), (CHUNKS - 1 if t == SETS - 1 else CHUNKS)

                def norm(p0, p1, s0, s1, k):
                    part = x_ring[p0:p1, q, s0:s1, :]
                    return act.activation(part, part, ACT.Identity, bias=gn_bias[p0:p1, k:k + 1], scale=gn_scale[p0:p1, k:k + 1])

                norm(0, P, lo, hi, 0)
                if lo == 0 and hi == CHUNKS:
                    norm(0, P, 8, 12, 1).then_inc(normed, 1)
                else:
                    out_main, out_rest, rows = (0, 8, slice(0, REST)) if lo else (CHUNKS - 1, 11, slice(REST, P))
                    norm(0, REST, 8 + lo, 12, 1)
                    norm(REST, P, 8, 4 + hi, 1)
                    act.copy(x_ring[:, q, out_main, :], zeros[:, :])
                    act.copy(x_ring[rows, q, out_rest, :], zeros[rows, :]).then_inc(normed, 1)

            def take_u1(b, i, c):
                T = SETS * b + 4 * i + c
                for m in range(3):
                    if not first(i, c, 4):
                        act.wait_ge(conv1_done, 3 * (STEPS * b + 4 * i + c - 4) + m + 1)
                    for half in range(2):
                        act.wait_ge(u1_ready, 6 * T + 2 * m + half + 1)
                        act.activation(u1[:, m, c % 4, HALF * half:HALF * (half + 1), 1:W + 1],
                                       psum[:, 2 * half:2 * half + 2, :].rearrange("p k (s w) -> p (k s) w", s=2),
                                       ACT.Identity).then_inc(u1_evac, 1)

            def take_qk(b, i, c):
                n0 = 3 * (STEPS * b + 4 * i + c - 2)
                for m in range(3):
                    n = n0 + m
                    if m == 0 and not first(i, c, 3):
                        act.wait_ge(scores_ready, 8 * (STEPS * b + 4 * i + c - 2))
                    for j in range(4):
                        act.wait_ge(qkt_ready, 4 * n + j + 1)
                        act.activation(qk_t[:, j // 2, P * m:P * (m + 1), HALF * (j % 2):HALF * (j % 2 + 1)],
                                       psum[:, 4 + j % 2, :].rearrange("p (s c) -> p c s", s=HALF),
                                       ACT.Identity).then_inc(qkt_evac, 1)
                    if m == 0 and not first(i, c, 4):
                        act.wait_ge(sq_added, STEPS * b + 4 * i + c - 3)
                    if not (first(i, c, 3) and m == 0):
                        act.wait_ge(squared, n)
                    for s in range(CHUNKS):
                        ins = act.activation(junk[:, s, :], conv1[:, (c + m) % 2, s, :], ACT.Square,
                                             accum_out=sq_step[:, c % 2, m, s:s + 1])
                    ins.then_inc(squared, 1)

            def take_u2(b, i, c):
                T = SETS * b + 4 * i + c
                for g in range(6):
                    if g in (0, 4) and not first(i, c, 4):
                        act.wait_ge(conv2_done, 2 * (STEPS * b + 4 * i + c - 4) + g // 4 + 1)
                    act.wait_ge(u2_ready, 6 * T + g + 1)
                    u = u2_main[:, c % 4, 2 * g:2 * g + 2] if g < 4 else u2_rest[:, c % 4, 2 * g - 8:2 * g - 6]
                    act.activation(u[:, :, 1:W + 1], psum[:, g % 2, :].rearrange("p (s w) -> p s w", s=2),
                                   ACT.Identity).then_inc(u2_evac, 1)

            def take_attention(b, i, c):
                n = STEPS * b + 4 * i + c - 2
                if not first(i, c, 3):
                    act.wait_ge(ao_ready, 8 * n)
                for k in range(8):
                    xh, h0 = k // 4, 2 * (k % 4)
                    act.wait_ge(ot_ready, 8 * n + k + 1)
                    act.activation(o_t[:, xh, HC * h0:HC * (h0 + 2), :].rearrange("p c s -> p (c s)"),
                                   psum[:, 2 + k % 2, 0:2 * L],
                                   ACT.Identity).then_inc(ot_evac, 1)
                if not first(i, c, 3):
                    act.wait_ge(proj_ready, 6 * n)
                for k in range(8):
                    act.wait_ge(ao_ready, 8 * n + k + 1)
                    ao = (ao_rest if k % 2 else ao_main)[:, k // 2 * 2:k // 2 * 2 + 2, :]
                    act.activation(ao, psum[REST * (k % 2):P, 4 + k % 2, :].rearrange("p (s w) -> p s w", s=2),
                                   ACT.Identity).then_inc(ao_evac, 1)

            with act.Fori(0, BATCH) as b:
                act.wait_ge(gn_dve, 5 * b + 3)
                act.activation(gn[:, 8:10], gn[:, 6:8], ACT.Sqrt).then_inc(gn_act, 1)
                act.wait_ge(gn_dve, 5 * b + 5)

                for c in range(3):
                    normalise(b, 0, c, x1_loaded, x1_normed)
                    take_u1(b, 0, c)
                normalise(b, 0, 3, x1_loaded, x1_normed)

                def step1(i, c):
                    if at(i, c) != SETS - 1:
                        take_u1(b, *move(i, c, 1))
                    if at(i, c) is None or at(i, c) + 2 < SETS:
                        normalise(b, *move(i, c, 2), x1_loaded, x1_normed)
                    take_qk(b, i, c)

                walk(act, step1)

                act.wait_ge(sq_added, STEPS * (b + 1))
                act.activation(nrm[:, 0], sumsq[:, :, :], ACT.Sqrt).then_inc(soft_act, 1)
                act.wait_ge(soft_dve, 5 * b + 3)
                for h in range(HEADS):
                    for g in range(2):
                        ins = act.activation(logits[:, h, g, :], logits[:, h, g, :], ACT.Exp, bias=soft[:, 1, h, g:g + 1],
                                             accum_out=soft[:, 2, h, g:g + 1])
                ins.then_inc(soft_act, 1)
                for k in range(8):
                    g, h0 = k // 4, 2 * (k % 4)
                    act.wait_ge(soft_pe, 8 * b + k + 1)
                    act.activation(attn_t[:, g, h0:h0 + 2, :], psum[0:LP, 4 + k % 2, 0:2 * L].rearrange("p (h n) -> p h n", h=2),
                                   ACT.Identity).then_inc(attn_t_evac, 1)

                for c in range(3):
                    normalise(b, 0, c, x2_loaded, x2_normed)
                    take_u2(b, 0, c)
                normalise(b, 0, 3, x2_loaded, x2_normed)

                def step2(i, c):
                    if at(i, c) != SETS - 1:
                        take_u2(b, *move(i, c, 1))
                    if at(i, c) is None or at(i, c) + 2 < SETS:
                        normalise(b, *move(i, c, 2), x2_loaded, x2_normed)
                    if not first(i, c, 3):
                        take_attention(b, *move(i, c, -1))

                walk(act, step2)
                take_attention(b, STEPS // 4 - 1, 5)

        @block.vector
        def _(dve):
            dve.wait_ge(zeroed, 1)

            def conv_tile(u, c, tap, acc, done, mac, base, between):
                for k, (dy, dx) in enumerate(TAPS):
                    src = u[:, (c + 2 + dy) % 4, :, dx:dx + W]
                    if k == 0:
                        ins = dve.tensor_scalar(acc, src, tap[:, 0:1], None, ALU.mult)
                    else:
                        dve.wait_ge(mac, base + k)
                        ins = dve.scalar_tensor_tensor(acc, src, tap[:, k:k + 1], acc, ALU.mult, ALU.add)
                    if k == 8:
                        ins.then_inc(done, 1)
                    else:
                        ins.then_inc(mac, 1)
                    between(k)

            with dve.Fori(0, BATCH) as b:
                def gn_chunk(k, q, count):
                    dve.wait_ge(gn_loaded[q], count)
                    for j in range(GN_CHUNK // BN):
                        ins = dve.bn_stats(bn[:, GN_CHUNK // BN * k + j, :], gn_in[q][:, BN * j:BN * (j + 1)])
                    ins.then_inc(gn_read, 1)

                with dve.Fori(0, GN_CHUNKS // 2) as i:
                    for q in range(2):
                        gn_chunk(2 * i + q, q, DMA * (GN_CHUNKS // 2 * b + i + 1))
                dve.wait_ge(gn_read, GN_CHUNKS * (b + 1))
                rows = u_mem[:, :].rearrange("p (r w) -> p r w", w=PAD)
                dve.memset(rows[:, :, 0:1], 0.0)
                dve.memset(rows[:, :, PAD - 1:PAD], 0.0)
                dve.memset(scores_mem[0:LP, :], 0.0)
                dve.memset(sumsq[:, :, :], 0.0).then_inc(sums_zeroed, 1)
                dve.bn_aggr(gn[:, 0:2], bn[:, :, :].rearrange("p k s -> p (k s)")).then_inc(gn_dve, 1)
                dve.wait_ge(gn_pe, 2 * b + 1)
                dve.tensor_copy(gn[:, 4:5], psum[:, 0, 0:1]).then_inc(gn_step, 1)
                dve.tensor_tensor(gn[:, 2:3], gn[:, 0:1], psum[:, 0, 0:1], ALU.subtract).then_inc(gn_step, 1)
                dve.wait_ge(gn_step, 6 * b + 2)
                dve.scalar_tensor_tensor(gn[:, 5:6], gn[:, 2:3], gn[:, 2:3], gn[:, 1:2], ALU.mult, ALU.add).then_inc(gn_dve, 1)
                dve.wait_ge(gn_pe, 2 * b + 2)
                group = psum[:, 1, 0:4].rearrange("p (k v) -> p v k", v=2)
                dve.tensor_scalar(gn[:, 6:8], group[:, 1], GN_EPS, None, ALU.add).then_inc(gn_dve, 1)
                dve.wait_ge(gn_act, b + 1)
                dve.reciprocal(gn[:, 10:12], gn[:, 8:10]).then_inc(gn_step, 1)
                dve.wait_ge(gn_step, 6 * b + 3)
                dve.tensor_tensor(gn[:, 10:12], gn[:, 10:12], gn[:, 6:8], ALU.mult).then_inc(gn_step, 1)
                dve.wait_ge(gn_step, 6 * b + 4)
                dve.tensor_tensor(gn[:, 10:12], gn[:, 10:12], gn[:, 8:10], ALU.add).then_inc(gn_step, 1)
                dve.wait_ge(gn_step, 6 * b + 5)
                dve.tensor_scalar(gn[:, 12:14], gn[:, 10:12], 0.5, None, ALU.mult).then_inc(gn_step, 1)
                dve.wait_ge(gn_step, 6 * b + 6)
                dve.reciprocal(gn_scale[:, :], gn[:, 12:14]).then_inc(gn_dve, 1)
                dve.wait_ge(gn_dve, 5 * b + 4)
                dve.scalar_tensor_tensor(gn_bias[:, :], gn_scale[:, :], -1.0, group[:, 0], ALU.mult, ALU.mult).then_inc(gn_dve, 1)

                def add_scores(i, c, h):
                    n = 8 * (STEPS * b + 4 * i + c - 2) + h
                    dve.wait_ge(scores_ready, n + 1)
                    dve.tensor_tensor(scores[:, h, :], scores[:, h, :], psum[0:LP, 6 + h % 2, 0:2 * L],
                                      ALU.add).then_inc(scores_added, 1)

                def step1(i, c):
                    T, n = SETS * b + 4 * i + c, STEPS * b + 4 * i + c - 2
                    for m in range(3):
                        dve.wait_ge(u1_evac, 6 * T + 2 * m + 2)
                        if not (first(i, c, 3) and m < 2):
                            dve.wait_ge(qkt_ready, 4 * (3 * n + m - 1))
                            dve.wait_ge(squared, 3 * n + m - 1)

                        def between(k, m=m):
                            if m == 0 and 0 < k and not first(i, c, 3):
                                add_scores(*move(i, c, -1), k - 1)

                        conv_tile(u1[:, m], c, taps[:, m], conv1[:, (c + m) % 2], conv1_done, mac1, 24 * n + 8 * m, between)

                walk(dve, step1)
                for h in range(HEADS):
                    add_scores(STEPS // 4 - 1, 5, h)

                def small(ins, k):
                    ins.then_inc(soft_step, 1)
                    dve.wait_ge(soft_step, 7 * b + k)

                dve.wait_ge(soft_act, 2 * b + 1)
                small(dve.tensor_scalar(nrm[:, 1], nrm[:, 0], NORM_EPS, None, ALU.max), 1)
                small(dve.reciprocal(nrm[:, 2], nrm[:, 1]), 2)
                small(dve.tensor_tensor(nrm[:, 2], nrm[:, 2], sumsq[:, :, :], ALU.mult), 3)
                small(dve.tensor_tensor(nrm[:, 2], nrm[:, 2], nrm[:, 1], ALU.add), 4)
                small(dve.tensor_scalar(nrm[:, 2], nrm[:, 2], 0.5, NORM_EPS, ALU.mult, ALU.max), 5)
                dve.reciprocal(nrm[:, 3], nrm[:, 2]).then_inc(soft_dve, 1)
                dve.wait_ge(soft_dma, DMA * 3 * (b + 1))
                small(dve.tensor_tensor(row_scale[:, :, :], row_scale[:, :, :],
                                        temp[:, :].rearrange("p (h o) -> p h o", o=1).to_broadcast([LP, HEADS, 2]), ALU.mult), 6)
                for h in range(HEADS):
                    for g in range(2):
                        ins = dve.scalar_tensor_tensor(logits[:, h, g, :], scores[:, h, L * g:L * (g + 1)],
                                                       row_scale[:, h, g:g + 1], k_scale[:, h, :], ALU.mult, ALU.mult)
                ins.then_inc(soft_dve, 1)
                dve.wait_ge(soft_dve, 5 * b + 2)
                small(dve.tensor_reduce(soft[:, 0], logits[:, :, :, :], AX_X, ALU.max), 7)
                dve.tensor_scalar(soft[:, 1], soft[:, 0], -1.0, None, ALU.mult).then_inc(soft_dve, 1)
                dve.wait_ge(soft_act, 2 * b + 2)
                dve.reciprocal(soft[:, 3], soft[:, 2]).then_inc(soft_dve, 1)
                dve.wait_ge(soft_dve, 5 * b + 4)
                flat = logits[:, :, :, :].rearrange("p h g n -> p (h g) n")
                dve.tensor_tensor(flat, flat, soft[:, 3].rearrange("p h (g o) -> p (h g) o", o=1).to_broadcast(
                    [LP, HEADS * 2, L]), ALU.mult).then_inc(soft_dve, 1)

                def add_resid(i, c, g):
                    q, n = c % 2, STEPS * b + 4 * i + c - 2
                    if g == 0:
                        dve.wait_ge(resid_loaded[q], 3 * DMA * (STEPS // 2 * b + 2 * i + (c - 2) // 2 + 1))
                    dve.wait_ge(proj_ready, 6 * n + g + 1)
                    part = resid[:, q, 2 * g:2 * g + 2, :]
                    dve.tensor_tensor(part, part, psum[:, 6 + g % 2, :].rearrange("p (s w) -> p s w", s=2),
                                      ALU.add).then_inc(resid_done, 1)

                def step2(i, c):
                    T, n = SETS * b + 4 * i + c, STEPS * b + 4 * i + c - 2
                    q = c % 2
                    if not first(i, c, 4):
                        dve.wait_ge(v_stored[q], 3 * DMA * (STEPS // 2 * b + 2 * i + (c - 2) // 2))
                    for m in range(2):
                        dve.wait_ge(u2_evac, 6 * T + (4, 6)[m])

                        def between(k, m=m):
                            g = 9 * m + k - 8
                            if 0 <= g < 6 and not first(i, c, 4):
                                add_resid(*move(i, c, -2), g)

                        conv_tile((u2_main, u2_rest)[m], c, taps[:, 3 + m], (v_main, v_rest)[m][:, q], conv2_done,
                                  mac2, 16 * n + 8 * m, between)

                walk(dve, step2)
                for c in (4, 5):
                    for g in range(6):
                        add_resid(STEPS // 4 - 1, c, g)
                for q in range(2):
                    dve.wait_ge(out_stored[q], 3 * DMA * STEPS // 2 * (b + 1))

        @block.gpsimd
        def _(pool):
            pool.memset(zeros[:, :], 0.0).then_inc(zeroed, 1)
            with pool.Fori(0, BATCH) as b:
                def step(i, c):
                    n = STEPS * b + 4 * i + c - 2
                    if first(i, c, 3):
                        pool.wait_ge(sums_zeroed, b + 1)
                    else:
                        pool.wait_ge(sq_added, n)
                    pool.wait_ge(squared, 3 * (n + 1))
                    pool.tensor_tensor(sumsq[:, :, :], sumsq[:, :, :], sq_step[:, c % 2], ALU.add).then_inc(sq_added, 1)

                walk(pool, step)


def kernel(x, L0_conv_qkv_w, L0_conv_dw_w, L0_conv_proj_w, L0_conv_temperature):
    import numpy as np
    import concourse.bacc as bacc
    from concourse.bass_utils import run_bass_kernel_spmd

    p = np.arange(P)
    ident = np.eye(P, dtype=np.float32)
    group_avg = np.where(p[:, None] // 4 == p[None, :] // 4, 0.25, 0.0).astype(np.float32)
    channel = np.stack([p, P + p % REST])
    per_group = C // GROUPS
    group_sel = np.where(p[:, None, None] // 4 == channel[None] // per_group, 0.25, 0.0).astype(np.float32)

    arrays = {
        "x_in": np.ascontiguousarray(x),
        "w_qkv_t": np.ascontiguousarray(np.asarray(L0_conv_qkv_w).T),
        "dw_in": np.ascontiguousarray(np.asarray(L0_conv_dw_w).reshape(3 * C, 9)),
        "proj_t": np.ascontiguousarray(np.asarray(L0_conv_proj_w).T),
        "temperature": np.ascontiguousarray(np.asarray(L0_conv_temperature).reshape(1, HEADS)),
        "ident_in": ident,
        "group_avg_in": group_avg,
        "group_sel_in": group_sel,
    }
    nc = bacc.Bacc("TRN2", target_bir_lowering=False, num_devices=1)
    args = [nc.dram_tensor(name, a.shape, mybir.dt.from_np(a.dtype), kind="ExternalInput").ap()
            for name, a in arrays.items()]
    out = nc.dram_tensor("out_dram", (BATCH, C, H, W), F32, kind="ExternalOutput").ap()
    conv_preact_kernel(nc, *args, out)
    r = run_bass_kernel_spmd(nc, [arrays], core_ids=[0])
    return r.results[0]["out_dram"]
```

```python
from contextlib import ExitStack

import concourse.bass as bass
from concourse import mybir

ALU = mybir.AluOpType
ACT = mybir.ActivationFunctionType
F32 = mybir.dt.float32
AX_X = mybir.AxisListType.X

P = 128
BATCH, C, H, W = 2, 192, 256, 256
HEADS, HC = 8, 24
CHUNKS = 8
RPC = H // CHUNKS
HALF = CHUNKS // 2
REST = C - P
L = HC * CHUNKS
LP = L // 2
SETS, STEPS = RPC + 2, RPC
PAD = W + 2
GROUPS = 32
GN_EPS, NORM_EPS = 1e-5, 1e-12
GN_CHUNK = 4096
GN_CHUNKS = C * H * W // P // GN_CHUNK
BN = 512
PE_CHUNKS = 4
PE_FILLS = PE_CHUNKS // 2
TAPS_FILL = 4
FILL = [0, TAPS_FILL + PE_FILLS, TAPS_FILL + PE_FILLS + 4]
FILLS = PE_FILLS + 12
ADD_SLOTS = [5, 6, 7, 7, 8, 8, 10, 10]
TAPS = [(dy, dx) for dy in range(3) for dx in range(3)]
BANK = 512
DMA = 16
CONSTS = 12


def conv_preact_kernel(nc, x, w_qkv_t, dw, proj_t, temperature, ident_in, group_avg_in, group_sel_in, out):
    inv_norms = nc.dram_tensor("inv_norms", [2 * C, CHUNKS], F32).ap()
    v_rows = nc.dram_tensor("v_rows", [2, C, CHUNKS, W], F32).ap()

    x_sets = x.rearrange("b c (s r) w -> b c s r w", s=CHUNKS)
    out_sets = out.rearrange("b c (s r) w -> b c s r w", s=CHUNKS)
    x_flat = x.rearrange("b c h w -> b (c h w)").rearrange("b (p k n) -> b p k n", p=P, n=GN_CHUNK)

    with ExitStack() as ctx:
        nc.disable_value_cache = True
        ctx.enter_context(nc.allow_non_contiguous_dma("norms of a few KB are permuted"))

        def sb(name, shape, dt=F32):
            return ctx.enter_context(nc.sbuf_tensor(name, shape, dt))

        def sem(name):
            return ctx.enter_context(nc.semaphore(name))

        w_main = sb("w_main", [P, 3 * C])
        w_rest = sb("w_rest", [P, 3 * C])
        taps = sb("taps", [P, 5, 9])
        proj_main = sb("proj_main", [P, C])
        proj_rest_mem = sb("proj_rest", [P, C])
        proj_rest = proj_rest_mem[REST:P, :]
        ident = sb("ident", [P, P])
        group_avg = sb("group_avg", [P, P])
        group_sel = sb("group_sel", [P, 2, P])
        temp = sb("temp", [LP, HEADS])
        zeros = sb("zeros", [P, 1])
        w_rest_v = sb("w_rest_v", [P, P])
        gn = sb("gn", [P, 16])
        gn_scale = sb("gn_scale", [P, 2])
        gn_bias = sb("gn_bias", [P, 2])
        sumsq = sb("sumsq", [P, 3, CHUNKS])
        sq_step = sb("sq_step", [P, 2, 3, CHUNKS])
        nrm = sb("nrm", [P, 4, 3, CHUNKS])
        row_scale = sb("row_scale", [LP, HEADS, 2])
        soft = sb("soft", [LP, 4, HEADS, 2])
        attn_mem = sb("attn_mem", [P, 2 * HEADS * L])
        diag = sb("diag", [P, 9, P])
        x_ring = sb("x_ring", [P, 2, 12, W])
        scores_mem = sb("scores_mem", [P, HEADS * 2 * L])
        u_mem = sb("u_mem", [P, 4 * 3 * CHUNKS * PAD])
        conv_mem = sb("conv_mem", [P, 3 * CHUNKS * W])
        qk_mem = sb("qk_mem", [P, CHUNKS * 2 * 2 * C])
        attn_t = attn_mem[0:LP, :].rearrange("p (g h n) -> p g h n", g=2, h=HEADS)
        junk = attn_mem[:, 0:CHUNKS * W].rearrange("p (s w) -> p s w", s=CHUNKS)

        gn_in = [conv_mem[:, 0:GN_CHUNK], qk_mem[:, 0:GN_CHUNK]]
        bn = qk_mem[:, GN_CHUNK:GN_CHUNK + GN_CHUNKS * (GN_CHUNK // BN) * 6].rearrange("p (k s) -> p k s", s=6)
        scores = scores_mem[0:LP, :].rearrange("p (h n) -> p h n", h=HEADS)
        u1 = u_mem[:, :].rearrange("p (m q s w) -> p m q s w", m=3, q=4, s=CHUNKS)
        conv1 = conv_mem[:, :].rearrange("p (m s w) -> p m s w", m=3, s=CHUNKS)
        qk_t = qk_mem[:, :].rearrange("p (x c s) -> p x c s", x=2, s=CHUNKS)
        logits = qk_mem[0:LP, 0:HEADS * 2 * L].rearrange("p (h g n) -> p h g n", h=HEADS, g=2)
        k_scale = conv_mem[0:LP, 0:HEADS * L].rearrange("p (h n) -> p h n", h=HEADS)
        t0, t1 = 4 * CHUNKS * PAD, 6 * CHUNKS * PAD
        u2_main = u1[:, 0]
        u2_rest = u_mem[:, t0:t1].rearrange("p (q s w) -> p q s w", q=4, s=HALF)
        o = t1
        resid = u_mem[:, o:o + 2 * 12 * W].rearrange("p (q s w) -> p q s w", q=2, s=12)
        o += 2 * 12 * W
        ao_main = u_mem[:, o:o + CHUNKS * W].rearrange("p (s w) -> p s w", s=CHUNKS)
        o += CHUNKS * W
        ao_rest = u_mem[REST:P, o:o + CHUNKS * W].rearrange("p (s w) -> p s w", s=CHUNKS)
        o += CHUNKS * W
        assert o <= 12 * CHUNKS * PAD
        v_main = conv1[:, 0:2]
        v_rest = qk_mem[:, 0:2 * HALF * W].rearrange("p (q s w) -> p q s w", q=2, s=HALF)
        o = 2 * HALF * W
        v_in = qk_mem[0:LP, o:o + 2 * HEADS * W].rearrange("p (h w) -> p h w", h=2 * HEADS)
        o_t = scores_mem[:, :].rearrange("p (x c s) -> p x c s", x=2, s=CHUNKS)

        psum = ctx.enter_context(nc.psum_tensor("psum", [P, 8, BANK], F32))

        consts_loaded = sem("consts_loaded")
        zeroed = sem("zeroed")
        diag_made = sem("diag_made")
        gn_loaded = [sem("gn_loaded0"), sem("gn_loaded1")]
        gn_read = sem("gn_read")
        gn_dve = sem("gn_dve")
        gn_pe = sem("gn_pe")
        gn_act = sem("gn_act")
        gn_step, soft_step = sem("gn_step"), sem("soft_step")
        sums_zeroed = sem("sums_zeroed")
        x1_loaded = [sem("x1_loaded0"), sem("x1_loaded1")]
        x1_normed = sem("x1_normed")
        u1_ready, u1_evac = sem("u1_ready"), sem("u1_evac")
        tap0_done = sem("tap0_done")
        mac1, conv1_done = sem("mac1"), sem("conv1_done")
        qkt_ready, qkt_evac = sem("qkt_ready"), sem("qkt_evac")
        squared, sq_added = sem("squared"), sem("sq_added")
        scores_ready, scores_added = sem("scores_ready"), sem("scores_added")
        soft_act, soft_dve, soft_pe, soft_dma = sem("soft_act"), sem("soft_dve"), sem("soft_pe"), sem("soft_dma")
        attn_t_evac = sem("attn_t_evac")
        x2_loaded = [sem("x2_loaded0"), sem("x2_loaded1")]
        x2_normed = sem("x2_normed")
        u2_ready, u2_evac = sem("u2_ready"), sem("u2_evac")
        mac2, conv2_done = sem("mac2"), sem("conv2_done")
        v_stored = [sem("v_stored0"), sem("v_stored1")]
        v_loaded = sem("v_loaded")
        ot_ready, ot_evac = sem("ot_ready"), sem("ot_evac")
        ao_ready, ao_evac = sem("ao_ready"), sem("ao_evac")
        proj_ready, resid_done = sem("proj_ready"), sem("resid_done")
        resid_loaded = [sem("resid_loaded0"), sem("resid_loaded1")]
        out_stored = [sem("out_stored0"), sem("out_stored1")]

        block = ctx.enter_context(nc.Block())

        def walk(eng, body):
            for c in range(2, 6):
                body(0, c)
            with eng.Fori(1, STEPS // 4 - 1) as i:
                for c in range(2, 6):
                    body(i, c)
            for c in range(2, 6):
                body(STEPS // 4 - 1, c)

        def first(i, c, t):
            return isinstance(i, int) and 4 * i + c < t

        def at(i, c):
            return 4 * i + c if isinstance(i, int) else None

        def move(i, c, by):
            return i, c + by

        @block.sync
        def _(sp):
            sp.dma_start(w_main[:, :], w_qkv_t[0:P, :]).then_inc(consts_loaded, DMA)
            for half in range(2):
                rows = slice(REST * half, REST * (half + 1))
                sp.dma_start(w_rest[rows, :], w_qkv_t[P:C, :]).then_inc(consts_loaded, DMA)
                sp.dma_start(taps[rows, 4, :], dw[2 * C + P:3 * C, :]).then_inc(consts_loaded, DMA)
            sp.dma_start(taps[:, 0:4, :], dw[0:4 * P, :].rearrange("(m p) k -> p m k", p=P)).then_inc(consts_loaded, DMA)
            sp.dma_start(proj_main[:, :], proj_t[0:P, :]).then_inc(consts_loaded, DMA)
            sp.dma_start(proj_rest, proj_t[P:C, :]).then_inc(consts_loaded, DMA)
            sp.dma_start(ident[:, :], ident_in[:, :]).then_inc(consts_loaded, DMA)
            sp.dma_start(group_avg[:, :], group_avg_in[:, :]).then_inc(consts_loaded, DMA)
            sp.dma_start(group_sel[:, :, :], group_sel_in[:, :, :]).then_inc(consts_loaded, DMA)
            sp.dma_start(temp[:, :], temperature[:, :].partition_broadcast(LP)).then_inc(consts_loaded, DMA)

            def load_set(b, i, c, loaded):
                t, q = at(i, c), c % 2
                sp.wait_ge(consts_loaded, CONSTS * DMA)
                lo, hi = (1 if t == 0 else 0), (CHUNKS - 1 if t == SETS - 1 else CHUNKS)
                if t == 0:
                    row = lambda c0, c1, s0, s1: x_sets[b, c0:c1, s0 - 1:s1 - 1, RPC - 1, :]
                elif t == SETS - 1:
                    row = lambda c0, c1, s0, s1: x_sets[b, c0:c1, s0 + 1:s1 + 1, 0, :]
                else:
                    row = lambda c0, c1, s0, s1: x_sets[b, c0:c1, s0:s1, 4 * i + c - 1, :]
                sp.dma_start(x_ring[:, q, lo:hi, :], row(0, P, lo, hi)).then_inc(loaded[q], DMA)
                sp.dma_start(x_ring[0:REST, q, 8 + lo:12, :], row(P, C, lo, HALF)).then_inc(loaded[q], DMA)
                sp.dma_start(x_ring[REST:P, q, 8:hi + 4, :], row(P, C, HALF, hi)).then_inc(loaded[q], DMA)

            with sp.Fori(0, BATCH) as b:
                def gn_load(k, q):
                    sp.wait_ge(consts_loaded, CONSTS * DMA)
                    sp.dma_start(gn_in[q], x_flat[b, :, k, :]).then_inc(gn_loaded[q], DMA)

                gn_load(0, 0)
                gn_load(1, 1)
                with sp.Fori(1, GN_CHUNKS // 2) as i:
                    for q in range(2):
                        sp.wait_ge(gn_read, b * GN_CHUNKS + 2 * i + q - 1)
                        gn_load(2 * i + q, q)

                load_set(b, 0, 0, x1_loaded)
                load_set(b, 0, 1, x1_loaded)

                def step1(i, c):
                    sp.wait_ge(u1_ready, 6 * (SETS * b + 4 * i + c - 1))
                    load_set(b, i, c, x1_loaded)

                walk(sp, step1)

                sp.wait_ge(soft_dve, 5 * b + 1)
                sp.dma_start(inv_norms.rearrange("(m p) s -> p m s", p=P), nrm[:, 3]).then_inc(soft_dma, DMA)
                sp.wait_ge(soft_dma, DMA * (3 * b + 1))
                q_norms = inv_norms[0:C, :].rearrange("c s -> (c s)").rearrange("(h g p) -> p h g", g=2, p=LP)
                sp.dma_start(row_scale[:, :, :], q_norms).then_inc(soft_dma, DMA)
                k_norms = inv_norms[C:2 * C, :].rearrange("(o c) s -> o (c s)", o=1)
                sp.dma_start(conv_mem[0:LP, 0:HEADS * L], k_norms.partition_broadcast(LP)).then_inc(soft_dma, DMA)

                def load_resid(i, c):
                    q = c % 2
                    r = 4 * i + c - 2
                    sp.wait_ge(consts_loaded, CONSTS * DMA)
                    sp.dma_start(resid[:, q, 0:8, :], x_sets[b, 0:P, :, r, :]).then_inc(resid_loaded[q], DMA)
                    sp.dma_start(resid[0:REST, q, 8:12, :], x_sets[b, P:C, 0:HALF, r, :]).then_inc(resid_loaded[q], DMA)
                    sp.dma_start(resid[REST:P, q, 8:12, :], x_sets[b, P:C, HALF:CHUNKS, r, :]).then_inc(resid_loaded[q], DMA)

                def store_v(i, c):
                    q = c % 2
                    sp.wait_ge(conv2_done, 2 * (STEPS * b + 4 * i + c - 1))
                    sp.dma_start(v_rows[q, 0:P], v_main[:, q]).then_inc(v_stored[q], DMA)
                    sp.dma_start(v_rows[q, P:C, 0:HALF], v_rest[0:REST, q]).then_inc(v_stored[q], DMA)
                    sp.dma_start(v_rows[q, P:C, HALF:CHUNKS], v_rest[REST:P, q]).then_inc(v_stored[q], DMA)

                def load_v(i, c):
                    q = c % 2
                    sp.wait_ge(v_stored[q], 3 * DMA * (STEPS // 2 * b + 2 * i + (c - 2) // 2 + 1))
                    if not first(i, c, 3):
                        sp.wait_ge(ot_ready, 8 * (STEPS * b + 4 * i + c - 2))
                    sp.dma_start(v_in, v_rows[q].rearrange("c s w -> (c s) w").rearrange("(h p) w -> p h w", p=LP)).then_inc(v_loaded, DMA)

                def store_out(i, c):
                    q, r = c % 2, 4 * i + c - 2
                    sp.wait_ge(resid_done, 6 * (STEPS * b + r + 1))
                    sp.wait_ge(consts_loaded, CONSTS * DMA)
                    sp.dma_start(out_sets[b, 0:P, :, r, :], resid[:, q, 0:8, :]).then_inc(out_stored[q], DMA)
                    sp.dma_start(out_sets[b, P:C, 0:HALF, r, :], resid[0:REST, q, 8:12, :]).then_inc(out_stored[q], DMA)
                    sp.dma_start(out_sets[b, P:C, HALF:CHUNKS, r, :], resid[REST:P, q, 8:12, :]).then_inc(out_stored[q], DMA)

                def load_next(i, c):
                    sp.wait_ge(u2_ready, 6 * (SETS * b + 4 * i + c + 1))
                    load_set(b, *move(i, c, 2), x2_loaded)

                load_set(b, 0, 0, x2_loaded)
                load_set(b, 0, 1, x2_loaded)
                load_resid(0, 2)
                load_resid(0, 3)

                for c in (0, 1):
                    load_next(0, c)

                def step2(i, c):
                    if at(i, c) is None or at(i, c) + 2 < SETS:
                        load_next(i, c)
                    if not first(i, c, 3):
                        store_v(*move(i, c, -1))
                        load_v(*move(i, c, -1))
                    if not first(i, c, 5):
                        j, d = move(i, c, -3)
                        store_out(j, d)
                        sp.wait_ge(out_stored[d % 2], 3 * DMA * (STEPS // 2 * b + 2 * j + (d - 2) // 2 + 1))
                        load_resid(j, d + 2)

                walk(sp, step2)
                last = STEPS // 4 - 1
                store_v(last, 5)
                load_v(last, 5)
                store_out(last, 3)
                sp.wait_ge(out_stored[1], 3 * DMA * (STEPS // 2 * b + 2 * last + 1))
                load_resid(last, 5)
                store_out(last, 4)
                store_out(last, 5)

            for q in range(2):
                sp.wait_ge(out_stored[q], 3 * DMA * STEPS // 2 * BATCH)

        @block.tensor
        def _(pe):
            pe.wait_ge(consts_loaded, CONSTS * DMA)

            def x_tile(q, s, n):
                half, l = s // HALF, s % HALF
                rows = slice(REST * half, REST * (half + 1))
                return x_ring[:, q, s:s + n, :], rows, x_ring[rows, q, 8 + l:8 + l + n, :]

            def first_conv1(b, i, c, parts):
                T = SETS * b + 4 * i + c
                for part in parts:
                    if part == 0:
                        pe.wait_ge(x1_normed, T + 1)
                    m, half, j = part // 4, part // 2 % 2, part % 2
                    g = 2 * m + half
                    if j == 0 and not (first(i, c, 1) and g < 2):
                        pe.wait_ge(u1_evac, 6 * T + g - 1)
                    x0, rows, x1 = x_tile(c % 2, HALF * half + 2 * j, 2)
                    bank = psum[:, 2 * half + j, :]
                    pe.matmul(bank, w_main[:, P * m:P * (m + 1)], x0, start=True, stop=False)
                    mm = pe.matmul(bank, w_rest[rows, P * m:P * (m + 1)], x1, start=False, stop=True)
                    if j == 1:
                        mm.then_inc(u1_ready, 1)

            def taps_on_pe(b, i, c):
                n = STEPS * b + 4 * i + c - 2
                for j in range(PE_FILLS):
                    pe.wait_ge(qkt_evac, FILLS * n + TAPS_FILL + j - 1)
                    for k, (dy, dx) in enumerate(TAPS):
                        mm = pe.matmul(psum[:, 4 + (c * FILLS + TAPS_FILL + j) % 2, :], diag[:, k, :],
                                       u1[:, 2, (c + 2 + dy) % 4, 2 * j:2 * j + 2, dx:dx + W], start=k == 0, stop=k == 8)
                    mm.then_inc(qkt_ready, 1)

            def transpose_qk(b, i, c, m, fills):
                n = STEPS * b + 4 * i + c - 2
                for j in fills:
                    if j == 0:
                        pe.wait_ge(conv1_done, 3 * n + m + 1)
                    fill = FILL[m] + j
                    if not (first(i, c, 3) and fill < 2):
                        pe.wait_ge(qkt_evac, FILLS * n + fill - 1)
                    for a in range(4):
                        mm = pe.transpose(psum[:, 4 + (c * FILLS + fill) % 2, P * a:P * (a + 1)],
                                          conv1[:, m, HALF * (j % 2) + a, P * (j // 2):P * (j // 2 + 1)], ident[:, :])
                    mm.then_inc(qkt_ready, 1)

            def head_rows(xh, c0):
                return qk_t[:, xh, c0:c0 + HC, :].rearrange("p j s -> p (j s)")

            def make_scores(b, i, c, heads):
                n = STEPS * b + 4 * i + c - 2
                for h in heads:
                    if h == 0:
                        pe.wait_ge(qkt_evac, FILLS * (n + 1))
                    if not (first(i, c, 3) and h < 2):
                        pe.wait_ge(scores_added, 8 * n + h - 1)
                    for g in range(2):
                        for xh in range(2):
                            mm = pe.matmul(psum[0:LP, 6 + h % 2, L * g:L * (g + 1)],
                                           head_rows(xh, HC * h)[:, LP * g:LP * (g + 1)],
                                           head_rows(xh, C + HC * h), start=xh == 0, stop=xh == 1)
                    mm.then_inc(scores_ready, 1)

            def first_conv2(b, i, c):
                T = SETS * b + 4 * i + c
                pe.wait_ge(x2_normed, T + 1)
                for g in range(6):
                    if not (first(i, c, 1) and g < 2):
                        pe.wait_ge(u2_evac, 6 * T + g - 1)
                    if g < 4:
                        x0, rows, x1 = x_tile(c % 2, 2 * g, 2)
                        bank = psum[:, g % 2, :]
                        pe.matmul(bank, w_main[:, 2 * C:2 * C + P], x0, start=True, stop=False)
                        mm = pe.matmul(bank, w_rest[rows, 2 * C:2 * C + P], x1, start=False, stop=True)
                    else:
                        l = 2 * (g - 4)
                        pe.matmul(psum[:, g % 2, :], w_rest_v[:, :], x_ring[:, c % 2, 8 + l:10 + l, :], start=True, stop=False)
                        for half in range(2):
                            x0, _, _ = x_tile(c % 2, HALF * half + l, 2)
                            mm = pe.matmul(psum[REST * half:REST * (half + 1), g % 2, :], w_main[:, 2 * C + P:3 * C], x0,
                                           start=False, stop=True)
                    mm.then_inc(u2_ready, 1)

            def attend(b, i, c):
                n = STEPS * b + 4 * i + c - 2
                pe.wait_ge(v_loaded, DMA * (n + 1))
                for k in range(8):
                    if not (first(i, c, 3) and k < 2):
                        pe.wait_ge(ot_evac, 8 * n + k - 1)
                    xh, h0 = k // 4, 2 * (k % 4)
                    for h in range(h0, h0 + 2):
                        for g in range(2):
                            mm = pe.matmul(psum[:, 2 + k % 2, L * (h - h0):L * (h - h0 + 1)],
                                           v_in[:, 2 * h + g, P * xh:P * (xh + 1)], attn_t[:, g, h, :], start=g == 0, stop=g == 1)
                    mm.then_inc(ot_ready, 1)
                pe.wait_ge(ot_evac, 8 * (n + 1))
                for k in range(8):
                    if not (first(i, c, 3) and k < 2):
                        pe.wait_ge(ao_evac, 8 * n + k - 1)
                    s, c0, c1 = 2 * (k // 2), REST * (k % 2), P + REST * (k % 2)
                    for a in range(4):
                        mm = pe.transpose(psum[:, 4 + k % 2, P * a:P * (a + 1)],
                                          o_t[:, a % 2, c0:c1, s + a // 2], ident[:, :])
                    mm.then_inc(ao_ready, 1)

            def project(b, i, c):
                n = STEPS * b + 4 * i + c - 2
                pe.wait_ge(ao_evac, 8 * (n + 1))
                for g in range(6):
                    if not (first(i, c, 3) and g < 2):
                        pe.wait_ge(resid_done, 6 * n + g - 1)
                    for half in ([0] if g < 4 else [0, 1]):
                        s = 2 * g if g < 4 else HALF * half + 2 * (g - 4)
                        rows, cols = (slice(0, P), slice(0, P)) if g < 4 else (
                            slice(REST * half, REST * (half + 1)), slice(P, C))
                        bank = psum[rows, 6 + g % 2, :]
                        pe.matmul(bank, proj_main[:, cols], ao_main[:, s:s + 2, :], start=True, stop=False)
                        mm = pe.matmul(bank, proj_rest[:, cols], ao_rest[:, s:s + 2, :], start=False, stop=True)
                    mm.then_inc(proj_ready, 1)

            with pe.Fori(0, BATCH) as b:
                pe.wait_ge(diag_made, 4)
                pe.wait_ge(gn_dve, 5 * b + 1)
                pe.matmul(psum[:, 0, 0:2], group_avg[:, :], gn[:, 0:2], start=True, stop=True).then_inc(gn_pe, 1)
                pe.wait_ge(gn_dve, 5 * b + 2)
                pe.matmul(psum[:, 1, 0:2], group_sel[:, 0, :], gn[:, 4:6], start=True, stop=True)
                pe.matmul(psum[:, 1, 2:4], group_sel[:, 1, :], gn[:, 4:6], start=True, stop=True).then_inc(gn_pe, 1)

                for c in range(3):
                    first_conv1(b, 0, c, range(12))

                def step1(i, c):
                    more, before = at(i, c) != SETS - 1, not first(i, c, 3)

                    def next_set(*parts):
                        if more:
                            first_conv1(b, *move(i, c, 1), parts)

                    for k in range(4):
                        if before:
                            transpose_qk(b, *move(i, c, -1), 1 + k // 2, (2 * (k % 2), 2 * (k % 2) + 1))
                        next_set(k)
                    for k in range(4):
                        if before:
                            make_scores(b, *move(i, c, -1), (2 * k, 2 * k + 1))
                        if k < 3:
                            next_set(4 + k)
                    transpose_qk(b, i, c, 0, (0, 1))
                    next_set(7)
                    transpose_qk(b, i, c, 0, (2, 3))
                    next_set(8, 9, 10, 11)
                    taps_on_pe(b, i, c)

                walk(pe, step1)
                for m in (1, 2):
                    transpose_qk(b, STEPS // 4 - 1, 5, m, range(4))
                make_scores(b, STEPS // 4 - 1, 5, range(HEADS))

                pe.wait_ge(soft_dve, 5 * b + 5)
                for k in range(8):
                    g, h0 = k // 4, 2 * (k % 4)
                    if k >= 2:
                        pe.wait_ge(attn_t_evac, 8 * b + k - 1)
                    for h in range(h0, h0 + 2):
                        for gq in range(2):
                            mm = pe.transpose(psum[0:LP, 4 + k % 2, L * (h - h0) + LP * gq:L * (h - h0) + LP * (gq + 1)],
                                              logits[:, h, gq, LP * g:LP * (g + 1)], ident[0:LP, 0:LP])
                    mm.then_inc(soft_pe, 1)
                pe.wait_ge(attn_t_evac, 8 * (b + 1))

                for c in range(3):
                    first_conv2(b, 0, c)

                def step2(i, c):
                    if at(i, c) != SETS - 1:
                        first_conv2(b, *move(i, c, 1))
                    if not first(i, c, 4):
                        project(b, *move(i, c, -2))
                    if not first(i, c, 3):
                        attend(b, *move(i, c, -1))

                walk(pe, step2)
                last = STEPS // 4 - 1
                project(b, last, 4)
                attend(b, last, 5)
                project(b, last, 5)

        @block.scalar
        def _(act):
            act.wait_ge(zeroed, 1)

            def normalise(b, i, c, loaded, normed):
                t, q = at(i, c), c % 2
                act.wait_ge(loaded[q], 3 * DMA * (SETS // 2 * b + 2 * i + c // 2 + 1))
                lo, hi = (1 if t == 0 else 0), (CHUNKS - 1 if t == SETS - 1 else CHUNKS)

                def norm(p0, p1, s0, s1, k):
                    part = x_ring[p0:p1, q, s0:s1, :]
                    return act.activation(part, part, ACT.Identity, bias=gn_bias[p0:p1, k:k + 1], scale=gn_scale[p0:p1, k:k + 1])

                norm(0, P, lo, hi, 0)
                if lo == 0 and hi == CHUNKS:
                    norm(0, P, 8, 12, 1).then_inc(normed, 1)
                else:
                    out_main, out_rest, rows = (0, 8, slice(0, REST)) if lo else (CHUNKS - 1, 11, slice(REST, P))
                    norm(0, REST, 8 + lo, 12, 1)
                    norm(REST, P, 8, 4 + hi, 1)
                    act.copy(x_ring[:, q, out_main, :], zeros[:, :].to_broadcast([P, W]))
                    act.copy(x_ring[rows, q, out_rest, :], zeros[rows, :].to_broadcast([REST, W])).then_inc(normed, 1)

            def take_u1(b, i, c, groups):
                T = SETS * b + 4 * i + c
                for g in groups:
                    m, half = g // 2, g % 2
                    if half == 0 and not first(i, c, 4):
                        act.wait_ge(conv1_done, 3 * (STEPS * b + 4 * i + c - 4) + m + 1)
                        if m == 2:
                            act.wait_ge(qkt_ready, FILLS * (STEPS * b + 4 * i + c - 4) + TAPS_FILL + PE_FILLS)
                    act.wait_ge(u1_ready, 6 * T + g + 1)
                    act.activation(u1[:, m, c % 4, HALF * half:HALF * (half + 1), 1:W + 1],
                                   psum[:, 2 * half:2 * half + 2, :].rearrange("p k (s w) -> p (k s) w", s=2),
                                   ACT.Identity).then_inc(u1_evac, 1)

            def take_taps(b, i, c):
                n = STEPS * b + 4 * i + c - 2
                if not first(i, c, 3):
                    act.wait_ge(squared, 3 * n)
                for j in range(PE_FILLS):
                    act.wait_ge(qkt_ready, FILLS * n + TAPS_FILL + j + 1)
                    act.activation(conv1[:, 2, 2 * j:2 * j + 2, :],
                                   psum[:, 4 + (c * FILLS + TAPS_FILL + j) % 2, :].rearrange("p (s w) -> p s w", s=2),
                                   ACT.Identity).then_inc(qkt_evac, 1)

            def take_qk(b, i, c, m, fills):
                n = STEPS * b + 4 * i + c - 2
                for j in fills:
                    if m == 0 and j == 0 and not first(i, c, 3):
                        act.wait_ge(scores_ready, 8 * n)
                    act.wait_ge(qkt_ready, FILLS * n + FILL[m] + j + 1)
                    act.activation(qk_t[:, j // 2, P * m:P * (m + 1), HALF * (j % 2):HALF * (j % 2 + 1)],
                                   psum[:, 4 + (c * FILLS + FILL[m] + j) % 2, :].rearrange("p (s c) -> p c s", s=HALF),
                                   ACT.Identity).then_inc(qkt_evac, 1)

            def tap0(b, i, c, m):
                n = STEPS * b + 4 * i + c - 2
                act.wait_ge(u1_evac, 6 * (SETS * b + 4 * i + c - 2) + 2 * m + 2)
                if not first(i, c, 3):
                    act.wait_ge(qkt_ready, FILLS * (n - 1) + FILL[m] + 4)
                    act.wait_ge(squared, 3 * (n - 1) + m + 1)
                s0 = PE_CHUNKS if m == 2 else 0
                act.activation(conv1[:, m, s0:CHUNKS], u1[:, m, (c + 2) % 4, s0:CHUNKS, 0:W], ACT.Identity,
                               scale=taps[:, m, 0:1]).then_inc(tap0_done, 1)

            def square(b, i, c, m):
                n = STEPS * b + 4 * i + c - 2
                if m == 0 and not first(i, c, 4):
                    act.wait_ge(sq_added, n - 1)
                if not (first(i, c, 3) and m == 0):
                    act.wait_ge(squared, 3 * n + m)
                for s in range(CHUNKS):
                    ins = act.activation(junk[:, s, :], conv1[:, m, s, :], ACT.Square,
                                         accum_out=sq_step[:, c % 2, m, s:s + 1])
                ins.then_inc(squared, 1)

            def take_u2(b, i, c):
                T = SETS * b + 4 * i + c
                for g in range(6):
                    if g in (0, 4) and not first(i, c, 4):
                        act.wait_ge(conv2_done, 2 * (STEPS * b + 4 * i + c - 4) + g // 4 + 1)
                    act.wait_ge(u2_ready, 6 * T + g + 1)
                    u = u2_main[:, c % 4, 2 * g:2 * g + 2] if g < 4 else u2_rest[:, c % 4, 2 * g - 8:2 * g - 6]
                    act.activation(u[:, :, 1:W + 1], psum[:, g % 2, :].rearrange("p (s w) -> p s w", s=2),
                                   ACT.Identity).then_inc(u2_evac, 1)

            def take_attention(b, i, c):
                n = STEPS * b + 4 * i + c - 2
                if not first(i, c, 3):
                    act.wait_ge(ao_ready, 8 * n)
                for k in range(8):
                    xh, h0 = k // 4, 2 * (k % 4)
                    act.wait_ge(ot_ready, 8 * n + k + 1)
                    act.activation(o_t[:, xh, HC * h0:HC * (h0 + 2), :].rearrange("p c s -> p (c s)"),
                                   psum[:, 2 + k % 2, 0:2 * L],
                                   ACT.Identity).then_inc(ot_evac, 1)
                if not first(i, c, 3):
                    act.wait_ge(proj_ready, 6 * n)
                for k in range(8):
                    act.wait_ge(ao_ready, 8 * n + k + 1)
                    ao = (ao_rest if k % 2 else ao_main)[:, k // 2 * 2:k // 2 * 2 + 2, :]
                    act.activation(ao, psum[REST * (k % 2):P, 4 + k % 2, :].rearrange("p (s w) -> p s w", s=2),
                                   ACT.Identity).then_inc(ao_evac, 1)

            with act.Fori(0, BATCH) as b:
                act.wait_ge(gn_dve, 5 * b + 3)
                act.activation(gn[:, 8:10], gn[:, 6:8], ACT.Sqrt).then_inc(gn_act, 1)
                act.wait_ge(gn_dve, 5 * b + 5)

                act.wait_ge(sums_zeroed, b + 1)
                for c in range(3):
                    normalise(b, 0, c, x1_loaded, x1_normed)
                    take_u1(b, 0, c, range(6))
                    if c == 0:
                        tap0(b, 0, 2, 0)
                normalise(b, 0, 3, x1_loaded, x1_normed)

                def step1(i, c):
                    more, before = at(i, c) != SETS - 1, not first(i, c, 3)

                    def next_set(*groups):
                        if more:
                            take_u1(b, *move(i, c, 1), groups)

                    if before:
                        last = move(i, c, -1)
                        take_qk(b, *last, 1, range(4))
                        take_qk(b, *last, 2, (0, 1))
                    next_set(0)
                    if before:
                        take_qk(b, *last, 2, (2, 3))
                    next_set(1)
                    for m in (1, 2):
                        if before:
                            square(b, *last, m)
                        tap0(b, i, c, m)
                    next_set(2)
                    take_qk(b, i, c, 0, (0, 1))
                    next_set(3)
                    take_qk(b, i, c, 0, (2, 3))
                    square(b, i, c, 0)
                    if more:
                        tap0(b, *move(i, c, 1), 0)
                    next_set(4, 5)
                    if at(i, c) is None or at(i, c) + 2 < SETS:
                        normalise(b, *move(i, c, 2), x1_loaded, x1_normed)
                    take_taps(b, i, c)

                walk(act, step1)
                for m in (1, 2):
                    take_qk(b, STEPS // 4 - 1, 5, m, range(4))
                for m in (1, 2):
                    square(b, STEPS // 4 - 1, 5, m)

                act.wait_ge(sq_added, STEPS * (b + 1))
                act.activation(nrm[:, 0], sumsq[:, :, :], ACT.Sqrt).then_inc(soft_act, 1)
                act.wait_ge(soft_dve, 5 * b + 3)
                for h in range(HEADS):
                    for g in range(2):
                        ins = act.activation(logits[:, h, g, :], logits[:, h, g, :], ACT.Exp, bias=soft[:, 1, h, g:g + 1],
                                             accum_out=soft[:, 2, h, g:g + 1])
                ins.then_inc(soft_act, 1)
                for k in range(8):
                    g, h0 = k // 4, 2 * (k % 4)
                    act.wait_ge(soft_pe, 8 * b + k + 1)
                    act.activation(attn_t[:, g, h0:h0 + 2, :], psum[0:LP, 4 + k % 2, 0:2 * L].rearrange("p (h n) -> p h n", h=2),
                                   ACT.Identity).then_inc(attn_t_evac, 1)

                for c in range(3):
                    normalise(b, 0, c, x2_loaded, x2_normed)
                    take_u2(b, 0, c)
                normalise(b, 0, 3, x2_loaded, x2_normed)

                def step2(i, c):
                    if at(i, c) != SETS - 1:
                        take_u2(b, *move(i, c, 1))
                    if at(i, c) is None or at(i, c) + 2 < SETS:
                        normalise(b, *move(i, c, 2), x2_loaded, x2_normed)
                    if not first(i, c, 3):
                        take_attention(b, *move(i, c, -1))

                walk(act, step2)
                take_attention(b, STEPS // 4 - 1, 5)

        @block.vector
        def _(dve):
            dve.wait_ge(consts_loaded, CONSTS * DMA)
            for k in range(9):
                ins = dve.tensor_scalar(diag[:, k, :], ident[:, :], taps[:, 2, k:k + 1], None, ALU.mult)
            ins.then_inc(diag_made, 1)
            dve.memset(w_rest_v[:, :], 0.0).then_inc(diag_made, 1)
            dve.wait_ge(diag_made, 2)
            for half in range(2):
                rows = slice(REST * half, REST * (half + 1))
                dve.tensor_copy(w_rest_v[rows, rows], w_rest[rows, 2 * C + P:3 * C]).then_inc(diag_made, 1)

            def tap_sum(u, c, k, tap, acc, mac, done, before):
                dy, dx = TAPS[k]
                src = u[:, (c + 2 + dy) % 4, :, dx:dx + W]
                if k == 0:
                    ins = dve.tensor_scalar(acc, src, tap[:, 0:1], None, ALU.mult)
                else:
                    if before is not None:
                        dve.wait_ge(mac, before)
                    ins = dve.scalar_tensor_tensor(acc, src, tap[:, k:k + 1], acc, ALU.mult, ALU.add)
                ins.then_inc(*((done, 1) if k == 8 else (mac, 1)))

            with dve.Fori(0, BATCH) as b:
                def gn_chunk(k, q, count):
                    dve.wait_ge(gn_loaded[q], count)
                    for j in range(GN_CHUNK // BN):
                        ins = dve.bn_stats(bn[:, GN_CHUNK // BN * k + j, :], gn_in[q][:, BN * j:BN * (j + 1)])
                    ins.then_inc(gn_read, 1)

                with dve.Fori(0, GN_CHUNKS // 2) as i:
                    for q in range(2):
                        gn_chunk(2 * i + q, q, DMA * (GN_CHUNKS // 2 * b + i + 1))
                dve.wait_ge(gn_read, GN_CHUNKS * (b + 1))
                rows = u_mem[:, :].rearrange("p (r w) -> p r w", w=PAD)
                dve.memset(rows[:, :, 0:1], 0.0)
                dve.memset(rows[:, :, PAD - 1:PAD], 0.0)
                dve.memset(scores_mem[0:LP, :], 0.0)
                dve.memset(sumsq[:, :, :], 0.0).then_inc(sums_zeroed, 1)
                dve.bn_aggr(gn[:, 0:2], bn[:, :, :].rearrange("p k s -> p (k s)")).then_inc(gn_dve, 1)
                dve.wait_ge(gn_pe, 2 * b + 1)
                dve.tensor_copy(gn[:, 4:5], psum[:, 0, 0:1]).then_inc(gn_step, 1)
                dve.tensor_tensor(gn[:, 2:3], gn[:, 0:1], psum[:, 0, 0:1], ALU.subtract).then_inc(gn_step, 1)
                dve.wait_ge(gn_step, 6 * b + 2)
                dve.scalar_tensor_tensor(gn[:, 5:6], gn[:, 2:3], gn[:, 2:3], gn[:, 1:2], ALU.mult, ALU.add).then_inc(gn_dve, 1)
                dve.wait_ge(gn_pe, 2 * b + 2)
                group = psum[:, 1, 0:4].rearrange("p (k v) -> p v k", v=2)
                dve.tensor_scalar(gn[:, 6:8], group[:, 1], GN_EPS, None, ALU.add).then_inc(gn_dve, 1)
                dve.wait_ge(gn_act, b + 1)
                dve.reciprocal(gn[:, 10:12], gn[:, 8:10]).then_inc(gn_step, 1)
                dve.wait_ge(gn_step, 6 * b + 3)
                dve.tensor_tensor(gn[:, 10:12], gn[:, 10:12], gn[:, 6:8], ALU.mult).then_inc(gn_step, 1)
                dve.wait_ge(gn_step, 6 * b + 4)
                dve.tensor_tensor(gn[:, 10:12], gn[:, 10:12], gn[:, 8:10], ALU.add).then_inc(gn_step, 1)
                dve.wait_ge(gn_step, 6 * b + 5)
                dve.tensor_scalar(gn[:, 12:14], gn[:, 10:12], 0.5, None, ALU.mult).then_inc(gn_step, 1)
                dve.wait_ge(gn_step, 6 * b + 6)
                dve.reciprocal(gn_scale[:, :], gn[:, 12:14]).then_inc(gn_dve, 1)
                dve.wait_ge(gn_dve, 5 * b + 4)
                dve.scalar_tensor_tensor(gn_bias[:, :], gn_scale[:, :], -1.0, group[:, 0], ALU.mult, ALU.mult).then_inc(gn_dve, 1)

                def add_scores(i, c, h):
                    n = 8 * (STEPS * b + 4 * i + c - 2) + h
                    dve.wait_ge(scores_ready, n + 1)
                    dve.tensor_tensor(scores[:, h, :], scores[:, h, :], psum[0:LP, 6 + h % 2, 0:2 * L],
                                      ALU.add).then_inc(scores_added, 1)

                def step1(i, c):
                    T, n = SETS * b + 4 * i + c, STEPS * b + 4 * i + c - 2
                    own = u1[:, 2, :, PE_CHUNKS:CHUNKS], conv1[:, 2, PE_CHUNKS:CHUNKS]

                    def add_due(k):
                        for h in range(HEADS):
                            if ADD_SLOTS[h] == k and not first(i, c, 3):
                                add_scores(*move(i, c, -1), h)

                    def tap(m, k, before):
                        if k == 1:
                            dve.wait_ge(tap0_done, 3 * n + m + 1)
                        u_in, acc = (u1[:, m], conv1[:, m]) if m < 2 else own
                        tap_sum(u_in, c, k, taps[:, m], acc, mac1, conv1_done, None if k == 1 else 21 * n + before)

                    def sets_there(k, m):
                        if first(i, c, 3):
                            if k in (3, 6):
                                dve.wait_ge(u1_evac, 6 * (T - 2 + k // 3) + 2 * m + 2)
                        elif k == 1:
                            dve.wait_ge(u1_evac, 6 * T + 2 * m + 2)

                    for k in range(1, 9):
                        sets_there(k, 0)
                        tap(0, k, k - 1)
                        add_due(k)
                    for k in range(1, 9):
                        sets_there(k, 2)
                        tap(1, k, 7 + 2 * k - 3)
                        tap(2, k, 7 + 2 * k - 2)
                        add_due(9 + k)

                walk(dve, step1)
                for h in range(HEADS):
                    add_scores(STEPS // 4 - 1, 5, h)

                def small(ins, k):
                    ins.then_inc(soft_step, 1)
                    dve.wait_ge(soft_step, 7 * b + k)

                dve.wait_ge(soft_act, 2 * b + 1)
                small(dve.tensor_scalar(nrm[:, 1], nrm[:, 0], NORM_EPS, None, ALU.max), 1)
                small(dve.reciprocal(nrm[:, 2], nrm[:, 1]), 2)
                small(dve.tensor_tensor(nrm[:, 2], nrm[:, 2], sumsq[:, :, :], ALU.mult), 3)
                small(dve.tensor_tensor(nrm[:, 2], nrm[:, 2], nrm[:, 1], ALU.add), 4)
                small(dve.tensor_scalar(nrm[:, 2], nrm[:, 2], 0.5, NORM_EPS, ALU.mult, ALU.max), 5)
                dve.reciprocal(nrm[:, 3], nrm[:, 2]).then_inc(soft_dve, 1)
                dve.wait_ge(soft_dma, DMA * 3 * (b + 1))
                small(dve.tensor_tensor(row_scale[:, :, :], row_scale[:, :, :],
                                        temp[:, :].rearrange("p (h o) -> p h o", o=1).to_broadcast([LP, HEADS, 2]), ALU.mult), 6)
                for h in range(HEADS):
                    for g in range(2):
                        ins = dve.scalar_tensor_tensor(logits[:, h, g, :], scores[:, h, L * g:L * (g + 1)],
                                                       row_scale[:, h, g:g + 1], k_scale[:, h, :], ALU.mult, ALU.mult)
                ins.then_inc(soft_dve, 1)
                dve.wait_ge(soft_dve, 5 * b + 2)
                small(dve.tensor_reduce(soft[:, 0], logits[:, :, :, :], AX_X, ALU.max), 7)
                dve.tensor_scalar(soft[:, 1], soft[:, 0], -1.0, None, ALU.mult).then_inc(soft_dve, 1)
                dve.wait_ge(soft_act, 2 * b + 2)
                dve.reciprocal(soft[:, 3], soft[:, 2]).then_inc(soft_dve, 1)
                dve.wait_ge(soft_dve, 5 * b + 4)
                flat = logits[:, :, :, :].rearrange("p h g n -> p (h g) n")
                dve.tensor_tensor(flat, flat, soft[:, 3].rearrange("p h (g o) -> p (h g) o", o=1).to_broadcast(
                    [LP, HEADS * 2, L]), ALU.mult).then_inc(soft_dve, 1)

                def add_resid(i, c, g):
                    q, n = c % 2, STEPS * b + 4 * i + c - 2
                    if g == 0:
                        dve.wait_ge(resid_loaded[q], 3 * DMA * (STEPS // 2 * b + 2 * i + (c - 2) // 2 + 1))
                    dve.wait_ge(proj_ready, 6 * n + g + 1)
                    part = resid[:, q, 2 * g:2 * g + 2, :]
                    dve.tensor_tensor(part, part, psum[:, 6 + g % 2, :].rearrange("p (s w) -> p s w", s=2),
                                      ALU.add).then_inc(resid_done, 1)

                def step2(i, c):
                    T, n = SETS * b + 4 * i + c, STEPS * b + 4 * i + c - 2
                    q = c % 2
                    if not first(i, c, 4):
                        dve.wait_ge(v_stored[q], 3 * DMA * (STEPS // 2 * b + 2 * i + (c - 2) // 2))
                    for m in range(2):
                        for k in range(9):
                            if first(i, c, 3):
                                if k % 3 == 0:
                                    dve.wait_ge(u2_evac, 6 * (T - 2 + k // 3) + (4, 6)[m])
                            elif k == 0:
                                dve.wait_ge(u2_evac, 6 * T + (4, 6)[m])
                            tap_sum((u2_main, u2_rest)[m], c, k, taps[:, 3 + m], (v_main, v_rest)[m][:, q], mac2,
                                    conv2_done, 16 * n + 8 * m + k)
                            g = 9 * m + k - 8
                            if 0 <= g < 6 and not first(i, c, 4):
                                add_resid(*move(i, c, -2), g)

                walk(dve, step2)
                for c in (4, 5):
                    for g in range(6):
                        add_resid(STEPS // 4 - 1, c, g)
                for q in range(2):
                    dve.wait_ge(out_stored[q], 3 * DMA * STEPS // 2 * (b + 1))

        @block.gpsimd
        def _(pool):
            pool.memset(zeros[:, :], 0.0).then_inc(zeroed, 1)
            with pool.Fori(0, BATCH) as b:
                def step(i, c):
                    n = STEPS * b + 4 * i + c - 2
                    if first(i, c, 3):
                        pool.wait_ge(sums_zeroed, b + 1)
                    else:
                        pool.wait_ge(sq_added, n)
                    pool.wait_ge(squared, 3 * (n + 1))
                    pool.tensor_tensor(sumsq[:, :, :], sumsq[:, :, :], sq_step[:, c % 2], ALU.add).then_inc(sq_added, 1)

                walk(pool, step)


def kernel(x, L0_conv_qkv_w, L0_conv_dw_w, L0_conv_proj_w, L0_conv_temperature):
    import numpy as np
    import concourse.bacc as bacc
    from concourse.bass_utils import run_bass_kernel_spmd

    p = np.arange(P)
    ident = np.eye(P, dtype=np.float32)
    group_avg = np.where(p[:, None] // 4 == p[None, :] // 4, 0.25, 0.0).astype(np.float32)
    channel = np.stack([p, P + p % REST])
    per_group = C // GROUPS
    group_sel = np.where(p[:, None, None] // 4 == channel[None] // per_group, 0.25, 0.0).astype(np.float32)

    arrays = {
        "x_in": np.ascontiguousarray(x),
        "w_qkv_t": np.ascontiguousarray(np.asarray(L0_conv_qkv_w).T),
        "dw_in": np.ascontiguousarray(np.asarray(L0_conv_dw_w).reshape(3 * C, 9)),
        "proj_t": np.ascontiguousarray(np.asarray(L0_conv_proj_w).T),
        "temperature": np.ascontiguousarray(np.asarray(L0_conv_temperature).reshape(1, HEADS)),
        "ident_in": ident,
        "group_avg_in": group_avg,
        "group_sel_in": group_sel,
    }
    nc = bacc.Bacc("TRN2", target_bir_lowering=False, num_devices=1)
    args = [nc.dram_tensor(name, a.shape, mybir.dt.from_np(a.dtype), kind="ExternalInput").ap()
            for name, a in arrays.items()]
    out = nc.dram_tensor("out_dram", (BATCH, C, H, W), F32, kind="ExternalOutput").ap()
    conv_preact_kernel(nc, *args, out)
    r = run_bass_kernel_spmd(nc, [arrays], core_ids=[0])
    return r.results[0]["out_dram"]
```

```python
from contextlib import ExitStack

import concourse.bass as bass
from concourse import mybir

ALU = mybir.AluOpType
ACT = mybir.ActivationFunctionType
F32 = mybir.dt.float32
AX_X = mybir.AxisListType.X

P = 128
BATCH, C, H, W = 2, 192, 256, 256
HEADS, HC = 8, 24
CHUNKS = 8
RPC = H // CHUNKS
HALF = CHUNKS // 2
REST = C - P
L = HC * CHUNKS
LP = L // 2
SETS, STEPS = RPC + 2, RPC
PAD = W + 2
GROUPS = 32
GN_EPS, NORM_EPS = 1e-5, 1e-12
GN_CHUNK = 4096
GN_CHUNKS = C * H * W // P // GN_CHUNK
GN_RING = 4
NEXT_CHUNK, NEXT_SLOTS = 1024, 3
NEXT_AT = [2, 4, 6]
BN = 512
PE_CHUNKS = 4
PE_FILLS = PE_CHUNKS // 2
TAPS_FILL = 4
FILL = [0, TAPS_FILL + PE_FILLS, TAPS_FILL + PE_FILLS + 4]
FILLS = PE_FILLS + 12
ADD_SLOTS = [5, 6, 7, 7, 8, 8, 10, 10]
RESID_SLOTS = [8, 10, 11, 12, 13, 14]
V_PLAN = [2, 1, 1, 1, 1]
NORM_AT = [2, 4, 6]
TAPS = [(dy, dx) for dy in range(3) for dx in range(3)]
BANK = 512
DMA = 16
CONSTS = 13


def conv_preact_kernel(nc, x, w_qkv_t, dw, proj_t, temperature, ident_in, group_avg_in, group_sel_in, out):
    inv_norms = nc.dram_tensor("inv_norms", [2 * C, CHUNKS], F32).ap()
    v_rows = nc.dram_tensor("v_rows", [2, C, CHUNKS, W], F32).ap()

    x_sets = x.rearrange("b c (s r) w -> b c s r w", s=CHUNKS)
    out_sets = out.rearrange("b c (s r) w -> b c s r w", s=CHUNKS)
    x_flat = x.rearrange("b c h w -> b (c h w)").rearrange("b (p k n) -> b p k n", p=P, n=GN_CHUNK)
    x_flat_next = x.rearrange("b c h w -> b (c h w)").rearrange("b (p k n) -> b p k n", p=P, n=NEXT_CHUNK)

    with ExitStack() as ctx:
        nc.disable_value_cache = True
        ctx.enter_context(nc.allow_non_contiguous_dma("norms of a few KB are permuted"))

        def sb(name, shape, dt=F32):
            return ctx.enter_context(nc.sbuf_tensor(name, shape, dt))

        def sem(name):
            return ctx.enter_context(nc.semaphore(name))

        w_main = sb("w_main", [P, 3 * C])
        w_rest = sb("w_rest", [P, 3 * C])
        taps = sb("taps", [P, 5, 9])
        proj_main = sb("proj_main", [P, C])
        proj_rest = sb("proj_rest", [P, C])
        ident = sb("ident", [P, P])
        group_avg = sb("group_avg", [P, P])
        group_sel = sb("group_sel", [P, 2, P])
        temp = sb("temp", [LP, HEADS])
        zeros = sb("zeros", [P, 1])
        w_rest_v = sb("w_rest_v", [P, P])
        proj_rest2 = sb("proj_rest2", [P, P])
        gn = sb("gn", [P, 16])
        gn_scale = sb("gn_scale", [P, 2])
        gn_bias = sb("gn_bias", [P, 2])
        sumsq = sb("sumsq", [P, 3, CHUNKS])
        sq_step = sb("sq_step", [P, 2, 3, CHUNKS])
        nrm = sb("nrm", [P, 4, 3, CHUNKS])
        row_scale = sb("row_scale", [LP, HEADS, 2])
        soft = sb("soft", [LP, 4, HEADS, 2])
        diag = sb("diag", [P, 9, P])
        x_ring = sb("x_ring", [P, 2, 12, W])
        scores_attn_mem = sb("scores_attn_mem", [P, 2 * HEADS * 2 * L])
        scores_mem, attn_mem = scores_attn_mem[:, 0:HEADS * 2 * L], scores_attn_mem[:, HEADS * 2 * L:]
        u_mem = sb("u_mem", [P, 4 * 3 * CHUNKS * PAD])
        conv_mem = sb("conv_mem", [P, 3 * CHUNKS * W])
        qk_mem = sb("qk_mem", [P, CHUNKS * 2 * 2 * C])
        attn_t = attn_mem[0:LP, :].rearrange("p (g h n) -> p g h n", g=2, h=HEADS)
        junk = attn_mem[:, 0:CHUNKS * W].rearrange("p (s w) -> p s w", s=CHUNKS)

        gn_in = [conv_mem[:, 0:GN_CHUNK], qk_mem[:, 0:GN_CHUNK], u_mem[:, 0:GN_CHUNK], u_mem[:, GN_CHUNK:2 * GN_CHUNK]]
        bn_end = 12 * CHUNKS * PAD
        bn_start = bn_end - C * H * W // P // BN * 6
        bn = u_mem[:, bn_start:bn_end].rearrange("p (k s) -> p k s", s=6)
        scores = scores_mem[0:LP, :].rearrange("p (h n) -> p h n", h=HEADS)
        u1 = u_mem[:, :].rearrange("p (m q s w) -> p m q s w", m=3, q=4, s=CHUNKS)
        conv1 = conv_mem[:, :].rearrange("p (m s w) -> p m s w", m=3, s=CHUNKS)
        qk_t = qk_mem[:, :].rearrange("p (x c s) -> p x c s", x=2, s=CHUNKS)
        logits = qk_mem[0:LP, 0:HEADS * 2 * L].rearrange("p (h g n) -> p h g n", h=HEADS, g=2)
        k_scale = conv_mem[0:LP, 0:HEADS * L].rearrange("p (h n) -> p h n", h=HEADS)
        t0, t1 = 4 * CHUNKS * PAD, 6 * CHUNKS * PAD
        u2_main = u1[:, 0]
        u2_rest = u_mem[:, t0:t1].rearrange("p (q s w) -> p q s w", q=4, s=HALF)
        o = t1
        resid = u_mem[:, o:o + 2 * 12 * W].rearrange("p (q s w) -> p q s w", q=2, s=12)
        o += 2 * 12 * W
        ao_main = u_mem[:, o:o + CHUNKS * W].rearrange("p (s w) -> p s w", s=CHUNKS)
        o += CHUNKS * W
        ao_rest = u_mem[:, o:o + HALF * W].rearrange("p (s w) -> p s w", s=HALF)
        o += HALF * W
        assert o + NEXT_CHUNK <= bn_start
        gn_next_in = [conv_mem[:, 2 * CHUNKS * W:2 * CHUNKS * W + NEXT_CHUNK],
                      conv_mem[:, 2 * CHUNKS * W + NEXT_CHUNK:2 * CHUNKS * W + 2 * NEXT_CHUNK],
                      u_mem[:, o:o + NEXT_CHUNK]]
        v_main = conv1[:, 0:2]
        v_rest = qk_mem[:, 0:2 * HALF * W].rearrange("p (q s w) -> p q s w", q=2, s=HALF)
        o = 2 * HALF * W
        v_in = qk_mem[0:LP, o:o + 2 * HEADS * W].rearrange("p (h w) -> p h w", h=2 * HEADS)
        o_t = scores_mem[:, :].rearrange("p (x c s) -> p x c s", x=2, s=CHUNKS)

        psum = ctx.enter_context(nc.psum_tensor("psum", [P, 8, BANK], F32))

        consts_loaded = sem("consts_loaded")
        zeroed = sem("zeroed")
        diag_made, blocks_made = sem("diag_made"), sem("blocks_made")
        gn_loaded = [sem(f"gn_loaded{q}") for q in range(GN_RING)]
        gn_next_loaded = [sem(f"gn_next_loaded{q}") for q in range(NEXT_SLOTS)]
        gn_read = sem("gn_read")
        gn_dve = sem("gn_dve")
        gn_pe = sem("gn_pe")
        gn_act = sem("gn_act")
        gn_step, soft_step = sem("gn_step"), sem("soft_step")
        sums_zeroed, pads_zeroed = sem("sums_zeroed"), sem("pads_zeroed")
        x1_loaded = [sem("x1_loaded0"), sem("x1_loaded1")]
        x1_normed = sem("x1_normed")
        u1_ready, u1_evac = sem("u1_ready"), sem("u1_evac")
        tap0_done, v_tap0_done = sem("tap0_done"), sem("v_tap0_done")
        mac1, conv1_done = sem("mac1"), sem("conv1_done")
        qkt_ready, qkt_evac = sem("qkt_ready"), sem("qkt_evac")
        squared, sq_added = sem("squared"), sem("sq_added")
        scores_ready, scores_added = sem("scores_ready"), sem("scores_added")
        soft_act, soft_dve, soft_pe, soft_dma = sem("soft_act"), sem("soft_dve"), sem("soft_pe"), sem("soft_dma")
        attn_t_evac = sem("attn_t_evac")
        x2_loaded = [sem("x2_loaded0"), sem("x2_loaded1")]
        x2_normed = sem("x2_normed")
        u2_ready, u2_evac = sem("u2_ready"), sem("u2_evac")
        mac2, conv2_done = sem("mac2"), sem("conv2_done")
        v_stored = [sem("v_stored0"), sem("v_stored1")]
        v_loaded = sem("v_loaded")
        ot_ready, ot_evac = sem("ot_ready"), sem("ot_evac")
        ao_ready, ao_evac = sem("ao_ready"), sem("ao_evac")
        proj_ready, resid_done = sem("proj_ready"), sem("resid_done")
        resid_loaded = [sem("resid_loaded0"), sem("resid_loaded1")]
        out_stored = [sem("out_stored0"), sem("out_stored1")]

        block = ctx.enter_context(nc.Block())

        def walk(eng, body):
            for c in range(2, 6):
                body(0, c)
            with eng.Fori(1, STEPS // 4 - 1) as i:
                for c in range(2, 6):
                    body(i, c)
            for c in range(2, 6):
                body(STEPS // 4 - 1, c)

        def batches(eng, body):
            with eng.Fori(0, BATCH - 1) as b:
                body(b, True)
            body(BATCH - 1, False)

        def gn_read_before(b):
            return GN_CHUNKS + NEXT_SLOTS * STEPS * b

        def first(i, c, t):
            return isinstance(i, int) and 4 * i + c < t

        def at(i, c):
            return 4 * i + c if isinstance(i, int) else None

        def move(i, c, by):
            return i, c + by

        @block.sync
        def _(sp):
            def gn_load(k, q):
                sp.dma_start(gn_in[q], x_flat[0, :, k, :]).then_inc(gn_loaded[q], DMA)

            gn_load(0, 0)
            sp.dma_start(w_main[:, :], w_qkv_t[0:P, :]).then_inc(consts_loaded, DMA)
            for half in range(2):
                rows = slice(REST * half, REST * (half + 1))
                sp.dma_start(w_rest[rows, :], w_qkv_t[P:C, :]).then_inc(consts_loaded, DMA)
                sp.dma_start(proj_rest[rows, :], proj_t[P:C, :]).then_inc(consts_loaded, DMA)
                sp.dma_start(taps[rows, 4, :], dw[2 * C + P:3 * C, :]).then_inc(consts_loaded, DMA)
            sp.dma_start(taps[:, 0:4, :], dw[0:4 * P, :].rearrange("(m p) k -> p m k", p=P)).then_inc(consts_loaded, DMA)
            sp.dma_start(proj_main[:, :], proj_t[0:P, :]).then_inc(consts_loaded, DMA)
            sp.dma_start(ident[:, :], ident_in[:, :]).then_inc(consts_loaded, DMA)
            sp.dma_start(group_avg[:, :], group_avg_in[:, :]).then_inc(consts_loaded, DMA)
            sp.dma_start(group_sel[:, :, :], group_sel_in[:, :, :]).then_inc(consts_loaded, DMA)
            sp.dma_start(temp[:, :], temperature[:, :].partition_broadcast(LP)).then_inc(consts_loaded, DMA)

            for q in range(1, GN_RING):
                gn_load(q, q)

            def load_set(b, i, c, loaded):
                t, q = at(i, c), c % 2
                sp.wait_ge(consts_loaded, CONSTS * DMA)
                lo, hi = (1 if t == 0 else 0), (CHUNKS - 1 if t == SETS - 1 else CHUNKS)
                if t == 0:
                    row = lambda c0, c1, s0, s1: x_sets[b, c0:c1, s0 - 1:s1 - 1, RPC - 1, :]
                elif t == SETS - 1:
                    row = lambda c0, c1, s0, s1: x_sets[b, c0:c1, s0 + 1:s1 + 1, 0, :]
                else:
                    row = lambda c0, c1, s0, s1: x_sets[b, c0:c1, s0:s1, 4 * i + c - 1, :]
                sp.dma_start(x_ring[:, q, lo:hi, :], row(0, P, lo, hi)).then_inc(loaded[q], DMA)
                sp.dma_start(x_ring[0:REST, q, 8 + lo:12, :], row(P, C, lo, HALF)).then_inc(loaded[q], DMA)
                sp.dma_start(x_ring[REST:P, q, 8:hi + 4, :], row(P, C, HALF, hi)).then_inc(loaded[q], DMA)

            with sp.Fori(1, GN_CHUNKS // GN_RING) as i:
                for q in range(GN_RING):
                    sp.wait_ge(gn_read, GN_RING * (i - 1) + q + 1)
                    sp.wait_ge(consts_loaded, CONSTS * DMA)
                    gn_load(GN_RING * i + q, q)

            def batch(b, more):
                load_set(b, 0, 0, x1_loaded)
                load_set(b, 0, 1, x1_loaded)

                def step1(i, c):
                    sp.wait_ge(u1_ready, 6 * (SETS * b + 4 * i + c - 1))
                    load_set(b, i, c, x1_loaded)

                walk(sp, step1)
                sp.wait_ge(u1_ready, 6 * SETS * (b + 1))
                load_set(b, 0, 0, x2_loaded)
                load_set(b, 0, 1, x2_loaded)

                sp.wait_ge(soft_dve, 5 * b + 1)
                sp.dma_start(inv_norms.rearrange("(m p) s -> p m s", p=P), nrm[:, 3]).then_inc(soft_dma, DMA)
                sp.wait_ge(soft_dma, DMA * (3 * b + 1))
                q_norms = inv_norms[0:C, :].rearrange("c s -> (c s)").rearrange("(h g p) -> p h g", g=2, p=LP)
                sp.dma_start(row_scale[:, :, :], q_norms).then_inc(soft_dma, DMA)
                k_norms = inv_norms[C:2 * C, :].rearrange("(o c) s -> o (c s)", o=1)
                sp.dma_start(conv_mem[0:LP, 0:HEADS * L], k_norms.partition_broadcast(LP)).then_inc(soft_dma, DMA)

                def load_resid(i, c):
                    q = c % 2
                    r = 4 * i + c - 2
                    sp.wait_ge(consts_loaded, CONSTS * DMA)
                    sp.dma_start(resid[:, q, 0:8, :], x_sets[b, 0:P, :, r, :]).then_inc(resid_loaded[q], DMA)
                    sp.dma_start(resid[0:REST, q, 8:12, :], x_sets[b, P:C, 0:HALF, r, :]).then_inc(resid_loaded[q], DMA)
                    sp.dma_start(resid[REST:P, q, 8:12, :], x_sets[b, P:C, HALF:CHUNKS, r, :]).then_inc(resid_loaded[q], DMA)

                def load_next_gn(i, c):
                    for k in range(NEXT_SLOTS):
                        if not first(i, c, 3):
                            sp.wait_ge(gn_read, gn_read_before(b) + NEXT_SLOTS * (4 * i + c - 3) + k + 1)
                        sp.wait_ge(consts_loaded, CONSTS * DMA)
                        sp.dma_start(gn_next_in[k], x_flat_next[b + 1, :, NEXT_SLOTS * (4 * i + c - 2) + k, :]).then_inc(
                            gn_next_loaded[k], DMA)

                def store_v(i, c):
                    q = c % 2
                    sp.wait_ge(conv2_done, 2 * (STEPS * b + 4 * i + c - 1))
                    sp.dma_start(v_rows[q, 0:P], v_main[:, q]).then_inc(v_stored[q], DMA)
                    sp.dma_start(v_rows[q, P:C, 0:HALF], v_rest[0:REST, q]).then_inc(v_stored[q], DMA)
                    sp.dma_start(v_rows[q, P:C, HALF:CHUNKS], v_rest[REST:P, q]).then_inc(v_stored[q], DMA)

                def load_v(i, c):
                    q = c % 2
                    sp.wait_ge(v_stored[q], 3 * DMA * (STEPS // 2 * b + 2 * i + (c - 2) // 2 + 1))
                    if not first(i, c, 3):
                        sp.wait_ge(ot_ready, 8 * (STEPS * b + 4 * i + c - 2))
                    sp.dma_start(v_in, v_rows[q].rearrange("c s w -> (c s) w").rearrange("(h p) w -> p h w", p=LP)).then_inc(v_loaded, DMA)

                def store_out(i, c):
                    q, r = c % 2, 4 * i + c - 2
                    sp.wait_ge(resid_done, 6 * (STEPS * b + r + 1))
                    sp.wait_ge(consts_loaded, CONSTS * DMA)
                    sp.dma_start(out_sets[b, 0:P, :, r, :], resid[:, q, 0:8, :]).then_inc(out_stored[q], DMA)
                    sp.dma_start(out_sets[b, P:C, 0:HALF, r, :], resid[0:REST, q, 8:12, :]).then_inc(out_stored[q], DMA)
                    sp.dma_start(out_sets[b, P:C, HALF:CHUNKS, r, :], resid[REST:P, q, 8:12, :]).then_inc(out_stored[q], DMA)

                def load_next(i, c):
                    sp.wait_ge(u2_ready, 6 * (SETS * b + 4 * i + c + 1))
                    load_set(b, *move(i, c, 2), x2_loaded)

                load_resid(0, 2)
                load_resid(0, 3)

                for c in (0, 1):
                    load_next(0, c)
                if more:
                    load_next_gn(0, 2)

                def step2(i, c):
                    j, d = move(i, c, -3)
                    if not first(i, c, 3):
                        store_v(*move(i, c, -1))
                    if not first(i, c, 5):
                        store_out(j, d)
                    if not first(i, c, 3):
                        load_v(*move(i, c, -1))
                    if at(i, c) is None or at(i, c) + 2 < SETS:
                        load_next(i, c)
                    if not first(i, c, 5):
                        sp.wait_ge(out_stored[d % 2], 3 * DMA * (STEPS // 2 * b + 2 * j + (d - 2) // 2 + 1))
                        load_resid(j, d + 2)
                    if more and at(i, c) != SETS - 1:
                        load_next_gn(*move(i, c, 1))

                walk(sp, step2)
                last = STEPS // 4 - 1
                store_v(last, 5)
                load_v(last, 5)
                store_out(last, 3)
                sp.wait_ge(out_stored[1], 3 * DMA * (STEPS // 2 * b + 2 * last + 1))
                load_resid(last, 5)
                store_out(last, 4)
                store_out(last, 5)

            batches(sp, batch)
            for q in range(2):
                sp.wait_ge(out_stored[q], 3 * DMA * STEPS // 2 * BATCH)

        @block.tensor
        def _(pe):
            pe.wait_ge(consts_loaded, CONSTS * DMA)

            def x_tile(q, s, n):
                half, l = s // HALF, s % HALF
                rows = slice(REST * half, REST * (half + 1))
                return x_ring[:, q, s:s + n, :], rows, x_ring[rows, q, 8 + l:8 + l + n, :]

            def first_conv1(b, i, c, parts):
                T = SETS * b + 4 * i + c
                for part in parts:
                    if part == 0:
                        pe.wait_ge(x1_normed, T + 1)
                    m, half, j = part // 4, part // 2 % 2, part % 2
                    g = 2 * m + half
                    if j == 0 and not (first(i, c, 1) and g < 2):
                        pe.wait_ge(u1_evac, 6 * T + g - 1)
                    x0, rows, x1 = x_tile(c % 2, HALF * half + 2 * j, 2)
                    bank = psum[:, 2 * half + j, :]
                    pe.matmul(bank, w_main[:, P * m:P * (m + 1)], x0, start=True, stop=False)
                    mm = pe.matmul(bank, w_rest[rows, P * m:P * (m + 1)], x1, start=False, stop=True)
                    if j == 1:
                        mm.then_inc(u1_ready, 1)

            def taps_on_pe(b, i, c):
                n = STEPS * b + 4 * i + c - 2
                for j in range(PE_FILLS):
                    pe.wait_ge(qkt_evac, FILLS * n + TAPS_FILL + j - 1)
                    for k, (dy, dx) in enumerate(TAPS):
                        mm = pe.matmul(psum[:, 4 + (c * FILLS + TAPS_FILL + j) % 2, :], diag[:, k, :],
                                       u1[:, 2, (c + 2 + dy) % 4, 2 * j:2 * j + 2, dx:dx + W], start=k == 0, stop=k == 8)
                    mm.then_inc(qkt_ready, 1)

            def transpose_qk(b, i, c, m, fills):
                n = STEPS * b + 4 * i + c - 2
                for j in fills:
                    if j == 0:
                        pe.wait_ge(conv1_done, 3 * n + m + 1)
                    fill = FILL[m] + j
                    if not (first(i, c, 3) and fill < 2):
                        pe.wait_ge(qkt_evac, FILLS * n + fill - 1)
                    for a in range(4):
                        mm = pe.transpose(psum[:, 4 + (c * FILLS + fill) % 2, P * a:P * (a + 1)],
                                          conv1[:, m, HALF * (j % 2) + a, P * (j // 2):P * (j // 2 + 1)], ident[:, :])
                    mm.then_inc(qkt_ready, 1)

            def head_rows(xh, c0):
                return qk_t[:, xh, c0:c0 + HC, :].rearrange("p j s -> p (j s)")

            def make_scores(b, i, c, heads):
                n = STEPS * b + 4 * i + c - 2
                for h in heads:
                    if h == 0:
                        pe.wait_ge(qkt_evac, FILLS * (n + 1))
                    if not (first(i, c, 3) and h < 2):
                        pe.wait_ge(scores_added, 8 * n + h - 1)
                    for g in range(2):
                        for xh in range(2):
                            mm = pe.matmul(psum[0:LP, 6 + h % 2, L * g:L * (g + 1)],
                                           head_rows(xh, HC * h)[:, LP * g:LP * (g + 1)],
                                           head_rows(xh, C + HC * h), start=xh == 0, stop=xh == 1)
                    mm.then_inc(scores_ready, 1)

            def first_conv2(b, i, c, groups):
                T = SETS * b + 4 * i + c
                for g in groups:
                    if g == 0:
                        pe.wait_ge(x2_normed, T + 1)
                    if not (first(i, c, 1) and g < 2):
                        pe.wait_ge(u2_evac, 6 * T + g - 1)
                    if g < 4:
                        x0, rows, x1 = x_tile(c % 2, 2 * g, 2)
                        bank = psum[:, g % 2, :]
                        pe.matmul(bank, w_main[:, 2 * C:2 * C + P], x0, start=True, stop=False)
                        mm = pe.matmul(bank, w_rest[rows, 2 * C:2 * C + P], x1, start=False, stop=True)
                    else:
                        l = 2 * (g - 4)
                        pe.matmul(psum[:, g % 2, :], w_rest_v[:, :], x_ring[:, c % 2, 8 + l:10 + l, :], start=True, stop=False)
                        for half in range(2):
                            x0, _, _ = x_tile(c % 2, HALF * half + l, 2)
                            mm = pe.matmul(psum[REST * half:REST * (half + 1), g % 2, :], w_main[:, 2 * C + P:3 * C], x0,
                                           start=False, stop=True)
                    mm.then_inc(u2_ready, 1)

            def attend(b, i, c):
                n = STEPS * b + 4 * i + c - 2
                pe.wait_ge(v_loaded, DMA * (n + 1))
                for k in range(8):
                    if not (first(i, c, 3) and k < 2):
                        pe.wait_ge(ot_evac, 8 * n + k - 1)
                    xh, h0 = k // 4, 2 * (k % 4)
                    for h in range(h0, h0 + 2):
                        for g in range(2):
                            mm = pe.matmul(psum[:, 2 + k % 2, L * (h - h0):L * (h - h0 + 1)],
                                           v_in[:, 2 * h + g, P * xh:P * (xh + 1)], attn_t[:, g, h, :], start=g == 0, stop=g == 1)
                    mm.then_inc(ot_ready, 1)
            def transpose_ao(b, i, c, fills):
                n = STEPS * b + 4 * i + c - 2
                for k in fills:
                    if k == 0:
                        pe.wait_ge(ot_evac, 8 * (n + 1))
                    if not (first(i, c, 3) and k < 2):
                        pe.wait_ge(ao_evac, 8 * n + k - 1)
                    s = 2 * (k // 2)
                    c0 = 0 if k % 2 == 0 else P if s < HALF else REST
                    for a in range(4):
                        start = (C * (a % 2) + c0) * CHUNKS
                        cols = scores_attn_mem[:, start:start + P * CHUNKS].rearrange("p (c s) -> p c s", s=CHUNKS)
                        mm = pe.transpose(psum[:, 4 + k % 2, P * a:P * (a + 1)], cols[:, :, s + a // 2], ident[:, :])
                    mm.then_inc(ao_ready, 1)

            def project(b, i, c):
                n = STEPS * b + 4 * i + c - 2
                pe.wait_ge(ao_evac, 8 * (n + 1))
                for g in range(6):
                    if not (first(i, c, 3) and g < 2):
                        pe.wait_ge(resid_done, 6 * n + g - 1)
                    bank = psum[:, 6 + g % 2, :]
                    if g < 4:
                        half, l = g // 2, 2 * (g % 2)
                        rows = slice(REST * half, REST * (half + 1))
                        pe.matmul(bank, proj_main[:, 0:P], ao_main[:, 2 * g:2 * g + 2, :], start=True, stop=False)
                        mm = pe.matmul(bank, proj_rest[rows, 0:P], ao_rest[rows, l:l + 2, :], start=False, stop=True)
                    else:
                        l = 2 * (g - 4)
                        pe.matmul(bank, proj_rest2[:, :], ao_rest[:, l:l + 2, :], start=True, stop=False)
                        for half in range(2):
                            s = HALF * half + l
                            mm = pe.matmul(psum[REST * half:REST * (half + 1), 6 + g % 2, :], proj_main[:, P:C],
                                           ao_main[:, s:s + 2, :], start=False, stop=True)
                    mm.then_inc(proj_ready, 1)

            with pe.Fori(0, BATCH) as b:
                pe.wait_ge(diag_made, 1)
                pe.wait_ge(blocks_made, 2 + 4)
                pe.wait_ge(gn_dve, 5 * b + 1)
                pe.matmul(psum[:, 0, 0:2], group_avg[:, :], gn[:, 0:2], start=True, stop=True).then_inc(gn_pe, 1)
                pe.wait_ge(gn_dve, 5 * b + 2)
                pe.matmul(psum[:, 1, 0:2], group_sel[:, 0, :], gn[:, 4:6], start=True, stop=True)
                pe.matmul(psum[:, 1, 2:4], group_sel[:, 1, :], gn[:, 4:6], start=True, stop=True).then_inc(gn_pe, 1)

                for c in range(3):
                    first_conv1(b, 0, c, range(12))

                def step1(i, c):
                    more, before = at(i, c) != SETS - 1, not first(i, c, 3)

                    def next_set(*parts):
                        if more:
                            first_conv1(b, *move(i, c, 1), parts)

                    for k in range(4):
                        if before:
                            transpose_qk(b, *move(i, c, -1), 1 + k // 2, (2 * (k % 2), 2 * (k % 2) + 1))
                        next_set(k)
                    for k in range(4):
                        if before:
                            make_scores(b, *move(i, c, -1), (2 * k, 2 * k + 1))
                        if k < 3:
                            next_set(4 + k)
                    transpose_qk(b, i, c, 0, (0, 1))
                    next_set(7)
                    transpose_qk(b, i, c, 0, (2, 3))
                    next_set(8, 9, 10, 11)
                    taps_on_pe(b, i, c)

                walk(pe, step1)
                pe.wait_ge(u1_evac, 6 * SETS * (b + 1))
                first_conv2(b, 0, 0, range(4))
                for m in (1, 2):
                    transpose_qk(b, STEPS // 4 - 1, 5, m, range(4))
                make_scores(b, STEPS // 4 - 1, 5, range(HEADS))
                first_conv2(b, 0, 0, (4, 5))
                first_conv2(b, 0, 1, range(6))

                pe.wait_ge(soft_dve, 5 * b + 5)
                for k in range(8):
                    g, h0 = k // 4, 2 * (k % 4)
                    if k >= 2:
                        pe.wait_ge(attn_t_evac, 8 * b + k - 1)
                    for h in range(h0, h0 + 2):
                        for gq in range(2):
                            mm = pe.transpose(psum[0:LP, 4 + k % 2, L * (h - h0) + LP * gq:L * (h - h0) + LP * (gq + 1)],
                                              logits[:, h, gq, LP * g:LP * (g + 1)], ident[0:LP, 0:LP])
                    mm.then_inc(soft_pe, 1)
                pe.wait_ge(attn_t_evac, 8 * (b + 1))

                first_conv2(b, 0, 2, range(6))

                def step2(i, c):
                    groups = iter(range(6) if at(i, c) != SETS - 1 else ())

                    def next_set(n):
                        if at(i, c) != SETS - 1:
                            first_conv2(b, *move(i, c, 1), [next(groups) for _ in range(n)])

                    next_set(V_PLAN[0])
                    if not first(i, c, 4):
                        project(b, *move(i, c, -2))
                    if not first(i, c, 3):
                        attend(b, *move(i, c, -1))
                    next_set(V_PLAN[1])
                    for k in range(4):
                        if not first(i, c, 3):
                            transpose_ao(b, *move(i, c, -1), (2 * k, 2 * k + 1))
                        if k < 3:
                            next_set(V_PLAN[k + 2])
                    next_set(6 - sum(V_PLAN))

                walk(pe, step2)
                last = STEPS // 4 - 1
                project(b, last, 4)
                attend(b, last, 5)
                transpose_ao(b, last, 5, range(8))
                project(b, last, 5)

        @block.scalar
        def _(act):
            act.wait_ge(zeroed, 1)

            def normalise(b, i, c, loaded, normed, thirds=(0, 1, 2)):
                t, q = at(i, c), c % 2
                if 0 in thirds:
                    act.wait_ge(loaded[q], 3 * DMA * (SETS // 2 * b + 2 * i + c // 2 + 1))
                lo, hi = (1 if t == 0 else 0), (CHUNKS - 1 if t == SETS - 1 else CHUNKS)

                def norm(p0, p1, s0, s1, k):
                    part = x_ring[p0:p1, q, s0:s1, :]
                    return act.activation(part, part, ACT.Identity, bias=gn_bias[p0:p1, k:k + 1], scale=gn_scale[p0:p1, k:k + 1])

                if lo == 0 and hi == CHUNKS:
                    for k in thirds:
                        ins = norm(0, P, 4 * k, 4 * k + 4, k // 2)
                    if 2 in thirds:
                        ins.then_inc(normed, 1)
                else:
                    norm(0, P, lo, hi, 0)
                    out_main, out_rest, rows = (0, 8, slice(0, REST)) if lo else (CHUNKS - 1, 11, slice(REST, P))
                    norm(0, REST, 8 + lo, 12, 1)
                    norm(REST, P, 8, 4 + hi, 1)
                    act.copy(x_ring[:, q, out_main, :], zeros[:, :].to_broadcast([P, W]))
                    act.copy(x_ring[rows, q, out_rest, :], zeros[rows, :].to_broadcast([REST, W])).then_inc(normed, 1)

            def take_u1(b, i, c, groups):
                T = SETS * b + 4 * i + c
                for g in groups:
                    m, half = g // 2, g % 2
                    if half == 0 and not first(i, c, 4):
                        act.wait_ge(conv1_done, 3 * (STEPS * b + 4 * i + c - 4) + m + 1)
                        if m == 2:
                            act.wait_ge(qkt_ready, FILLS * (STEPS * b + 4 * i + c - 4) + TAPS_FILL + PE_FILLS)
                    act.wait_ge(u1_ready, 6 * T + g + 1)
                    act.activation(u1[:, m, c % 4, HALF * half:HALF * (half + 1), 1:W + 1],
                                   psum[:, 2 * half:2 * half + 2, :].rearrange("p k (s w) -> p (k s) w", s=2),
                                   ACT.Identity).then_inc(u1_evac, 1)

            def take_taps(b, i, c):
                n = STEPS * b + 4 * i + c - 2
                if not first(i, c, 3):
                    act.wait_ge(squared, 3 * n)
                for j in range(PE_FILLS):
                    act.wait_ge(qkt_ready, FILLS * n + TAPS_FILL + j + 1)
                    act.activation(conv1[:, 2, 2 * j:2 * j + 2, :],
                                   psum[:, 4 + (c * FILLS + TAPS_FILL + j) % 2, :].rearrange("p (s w) -> p s w", s=2),
                                   ACT.Identity).then_inc(qkt_evac, 1)

            def take_qk(b, i, c, m, fills):
                n = STEPS * b + 4 * i + c - 2
                for j in fills:
                    if m == 0 and j == 0 and not first(i, c, 3):
                        act.wait_ge(scores_ready, 8 * n)
                    act.wait_ge(qkt_ready, FILLS * n + FILL[m] + j + 1)
                    act.activation(qk_t[:, j // 2, P * m:P * (m + 1), HALF * (j % 2):HALF * (j % 2 + 1)],
                                   psum[:, 4 + (c * FILLS + FILL[m] + j) % 2, :].rearrange("p (s c) -> p c s", s=HALF),
                                   ACT.Identity).then_inc(qkt_evac, 1)

            def tap0(b, i, c, m):
                n = STEPS * b + 4 * i + c - 2
                act.wait_ge(u1_evac, 6 * (SETS * b + 4 * i + c - 2) + 2 * m + 2)
                if not first(i, c, 3):
                    act.wait_ge(qkt_ready, FILLS * (n - 1) + FILL[m] + 4)
                    act.wait_ge(squared, 3 * (n - 1) + m + 1)
                s0 = PE_CHUNKS if m == 2 else 0
                act.activation(conv1[:, m, s0:CHUNKS], u1[:, m, (c + 2) % 4, s0:CHUNKS, 0:W], ACT.Identity,
                               scale=taps[:, m, 0:1]).then_inc(tap0_done, 1)

            def square(b, i, c, m):
                n = STEPS * b + 4 * i + c - 2
                if m == 0 and not first(i, c, 4):
                    act.wait_ge(sq_added, n - 1)
                if not (first(i, c, 3) and m == 0):
                    act.wait_ge(squared, 3 * n + m)
                for s in range(CHUNKS):
                    ins = act.activation(junk[:, s, :], conv1[:, m, s, :], ACT.Square,
                                         accum_out=sq_step[:, c % 2, m, s:s + 1])
                ins.then_inc(squared, 1)

            def v_tap0(b, i, c):
                q = c % 2
                act.wait_ge(u2_evac, 6 * (SETS * b + 4 * i + c - 1))
                if not first(i, c, 4):
                    act.wait_ge(v_stored[q], 3 * DMA * (STEPS // 2 * b + 2 * i + (c - 2) // 2))
                for m in range(2):
                    act.activation((v_main, v_rest)[m][:, q], (u2_main, u2_rest)[m][:, (c + 2) % 4, :, 0:W], ACT.Identity,
                                   scale=taps[:, 3 + m, 0:1]).then_inc(v_tap0_done, 1)

            def take_u2(b, i, c, groups):
                T = SETS * b + 4 * i + c
                for g in groups:
                    if g in (0, 4) and not first(i, c, 4):
                        act.wait_ge(conv2_done, 2 * (STEPS * b + 4 * i + c - 4) + g // 4 + 1)
                    act.wait_ge(u2_ready, 6 * T + g + 1)
                    u = u2_main[:, c % 4, 2 * g:2 * g + 2] if g < 4 else u2_rest[:, c % 4, 2 * g - 8:2 * g - 6]
                    act.activation(u[:, :, 1:W + 1], psum[:, g % 2, :].rearrange("p (s w) -> p s w", s=2),
                                   ACT.Identity).then_inc(u2_evac, 1)

            def take_ot(b, i, c, fills):
                n = STEPS * b + 4 * i + c - 2
                for k in fills:
                    if k == 0 and not first(i, c, 3):
                        act.wait_ge(ao_ready, 8 * n)
                    xh, h0 = k // 4, 2 * (k % 4)
                    act.wait_ge(ot_ready, 8 * n + k + 1)
                    act.activation(o_t[:, xh, HC * h0:HC * (h0 + 2), :].rearrange("p c s -> p (c s)"),
                                   psum[:, 2 + k % 2, 0:2 * L],
                                   ACT.Identity).then_inc(ot_evac, 1)

            def take_ao(b, i, c, fills):
                n = STEPS * b + 4 * i + c - 2
                for k in fills:
                    if k == 0 and not first(i, c, 3):
                        act.wait_ge(proj_ready, 6 * n)
                    act.wait_ge(ao_ready, 8 * n + k + 1)
                    s = 2 * (k // 2)
                    if k % 2 == 0:
                        rows, ao = slice(0, P), ao_main[:, s:s + 2, :]
                    else:
                        rows = slice(REST * (s // HALF), REST * (s // HALF + 1))
                        ao = ao_rest[rows, s % HALF:s % HALF + 2, :]
                    act.activation(ao, psum[rows, 4 + k % 2, :].rearrange("p (s w) -> p s w", s=2),
                                   ACT.Identity).then_inc(ao_evac, 1)

            with act.Fori(0, BATCH) as b:
                act.wait_ge(gn_dve, 5 * b + 3)
                act.activation(gn[:, 8:10], gn[:, 6:8], ACT.Sqrt).then_inc(gn_act, 1)
                act.wait_ge(gn_dve, 5 * b + 5)

                act.wait_ge(pads_zeroed, b + 1)
                normalise(b, 0, 0, x1_loaded, x1_normed)
                normalise(b, 0, 1, x1_loaded, x1_normed)
                take_u1(b, 0, 0, range(6))
                tap0(b, 0, 2, 0)
                for c in (1, 2):
                    take_u1(b, 0, c, range(3))
                    normalise(b, 0, c + 1, x1_loaded, x1_normed)
                    take_u1(b, 0, c, range(3, 6))

                def step1(i, c):
                    more, before = at(i, c) != SETS - 1, not first(i, c, 3)

                    def next_set(*groups):
                        if more:
                            take_u1(b, *move(i, c, 1), groups)

                    if before:
                        last = move(i, c, -1)
                        take_qk(b, *last, 1, range(4))
                        take_qk(b, *last, 2, (0, 1))
                    next_set(0)
                    if before:
                        take_qk(b, *last, 2, (2, 3))
                    next_set(1)
                    for m in (1, 2):
                        if before:
                            square(b, *last, m)
                        tap0(b, i, c, m)
                    next_set(2)
                    take_qk(b, i, c, 0, (0, 1))
                    next_set(3)
                    take_qk(b, i, c, 0, (2, 3))
                    square(b, i, c, 0)
                    if more:
                        tap0(b, *move(i, c, 1), 0)
                    next_set(4, 5)
                    if at(i, c) is None or at(i, c) + 2 < SETS:
                        normalise(b, *move(i, c, 2), x1_loaded, x1_normed)
                    take_taps(b, i, c)

                walk(act, step1)
                normalise(b, 0, 0, x2_loaded, x2_normed)
                act.wait_ge(conv1_done, 3 * STEPS * (b + 1) - 2)
                take_u2(b, 0, 0, range(4))
                normalise(b, 0, 1, x2_loaded, x2_normed)
                for m in (1, 2):
                    take_qk(b, STEPS // 4 - 1, 5, m, range(4))
                for m in (1, 2):
                    square(b, STEPS // 4 - 1, 5, m)

                act.wait_ge(sq_added, STEPS * (b + 1))
                act.activation(nrm[:, 0], sumsq[:, :, :], ACT.Sqrt).then_inc(soft_act, 1)
                act.wait_ge(conv1_done, 3 * STEPS * (b + 1))
                take_u2(b, 0, 0, (4, 5))
                take_u2(b, 0, 1, range(6))
                act.wait_ge(soft_dve, 5 * b + 3)
                for h in range(HEADS):
                    for g in range(2):
                        ins = act.activation(logits[:, h, g, :], logits[:, h, g, :], ACT.Exp, bias=soft[:, 1, h, g:g + 1],
                                             accum_out=soft[:, 2, h, g:g + 1])
                ins.then_inc(soft_act, 1)
                normalise(b, 0, 2, x2_loaded, x2_normed)
                for k in range(8):
                    g, h0 = k // 4, 2 * (k % 4)
                    act.wait_ge(soft_pe, 8 * b + k + 1)
                    act.activation(attn_t[:, g, h0:h0 + 2, :], psum[0:LP, 4 + k % 2, 0:2 * L].rearrange("p (h n) -> p h n", h=2),
                                   ACT.Identity).then_inc(attn_t_evac, 1)

                v_tap0(b, 0, 2)
                take_u2(b, 0, 2, range(3))
                normalise(b, 0, 3, x2_loaded, x2_normed)
                take_u2(b, 0, 2, range(3, 6))

                def step2(i, c):
                    groups = iter(range(6))

                    def next_set(n):
                        if at(i, c) != SETS - 1:
                            take_u2(b, *move(i, c, 1), [next(groups) for _ in range(n)])

                    next_set(V_PLAN[0])
                    if at(i, c) != SETS - 1:
                        v_tap0(b, *move(i, c, 1))
                    full = at(i, c) is None or at(i, c) + 2 < SETS - 1
                    if not first(i, c, 3):
                        for k in range(8):
                            take_ot(b, *move(i, c, -1), (k,))
                            if full and k in NORM_AT:
                                normalise(b, *move(i, c, 2), x2_loaded, x2_normed, (NORM_AT.index(k),))
                    elif full:
                        normalise(b, *move(i, c, 2), x2_loaded, x2_normed)
                    if at(i, c) is not None and at(i, c) + 2 == SETS - 1:
                        normalise(b, *move(i, c, 2), x2_loaded, x2_normed)
                    next_set(V_PLAN[1])
                    for k in range(4):
                        if not first(i, c, 3):
                            take_ao(b, *move(i, c, -1), (2 * k, 2 * k + 1))
                        if k < 3:
                            next_set(V_PLAN[k + 2])
                    next_set(6 - sum(V_PLAN))

                walk(act, step2)
                take_ot(b, STEPS // 4 - 1, 5, range(8))
                take_ao(b, STEPS // 4 - 1, 5, range(8))

        @block.vector
        def _(dve):
            dve.wait_ge(consts_loaded, CONSTS * DMA)
            for k in range(9):
                ins = dve.tensor_scalar(diag[:, k, :], ident[:, :], taps[:, 2, k:k + 1], None, ALU.mult)
            ins.then_inc(diag_made, 1)
            dve.memset(w_rest_v[:, :], 0.0).then_inc(blocks_made, 1)
            dve.memset(proj_rest2[:, :], 0.0).then_inc(blocks_made, 1)
            dve.wait_ge(blocks_made, 2)
            for half in range(2):
                rows = slice(REST * half, REST * (half + 1))
                dve.tensor_copy(w_rest_v[rows, rows], w_rest[rows, 2 * C + P:3 * C]).then_inc(blocks_made, 1)
                dve.tensor_copy(proj_rest2[rows, rows], proj_rest[rows, P:C]).then_inc(blocks_made, 1)

            def tap_sum(u, c, k, tap, acc, mac, done, before):
                dy, dx = TAPS[k]
                if k > 1:
                    dve.wait_ge(mac, before)
                dve.scalar_tensor_tensor(acc, u[:, (c + 2 + dy) % 4, :, dx:dx + W], tap[:, k:k + 1], acc, ALU.mult,
                                         ALU.add).then_inc(*((done, 1) if k == 8 else (mac, 1)))

            def gn_stats(source, entry):
                for j in range(source.shape[1] // BN):
                    ins = dve.bn_stats(bn[:, entry + j, :], source[:, BN * j:BN * (j + 1)])
                ins.then_inc(gn_read, 1)

            with dve.Fori(0, GN_CHUNKS // GN_RING) as i:
                for q in range(GN_RING):
                    dve.wait_ge(gn_loaded[q], DMA * (i + 1))
                    gn_stats(gn_in[q], GN_CHUNK // BN * (GN_RING * i + q))

            def batch(b, more):
                dve.wait_ge(gn_read, gn_read_before(b))
                dve.memset(sumsq[:, :, :], 0.0)
                dve.bn_aggr(gn[:, 0:2], bn[:, :, :].rearrange("p k s -> p (k s)")).then_inc(gn_dve, 1)
                dve.memset(scores_mem[0:LP, :], 0.0).then_inc(sums_zeroed, 1)
                dve.wait_ge(gn_dve, 5 * b + 1)
                rows = u_mem[:, :].rearrange("p (r w) -> p r w", w=PAD)
                dve.memset(rows[:, :, 0:1], 0.0)
                dve.memset(rows[:, :, PAD - 1:PAD], 0.0).then_inc(pads_zeroed, 1)
                dve.wait_ge(gn_pe, 2 * b + 1)
                dve.tensor_copy(gn[:, 4:5], psum[:, 0, 0:1]).then_inc(gn_step, 1)
                dve.tensor_tensor(gn[:, 2:3], gn[:, 0:1], psum[:, 0, 0:1], ALU.subtract).then_inc(gn_step, 1)
                dve.wait_ge(gn_step, 6 * b + 2)
                dve.scalar_tensor_tensor(gn[:, 5:6], gn[:, 2:3], gn[:, 2:3], gn[:, 1:2], ALU.mult, ALU.add).then_inc(gn_dve, 1)
                dve.wait_ge(gn_pe, 2 * b + 2)
                group = psum[:, 1, 0:4].rearrange("p (k v) -> p v k", v=2)
                dve.tensor_scalar(gn[:, 6:8], group[:, 1], GN_EPS, None, ALU.add).then_inc(gn_dve, 1)
                dve.wait_ge(gn_act, b + 1)
                dve.reciprocal(gn[:, 10:12], gn[:, 8:10]).then_inc(gn_step, 1)
                dve.wait_ge(gn_step, 6 * b + 3)
                dve.tensor_tensor(gn[:, 10:12], gn[:, 10:12], gn[:, 6:8], ALU.mult).then_inc(gn_step, 1)
                dve.wait_ge(gn_step, 6 * b + 4)
                dve.tensor_tensor(gn[:, 10:12], gn[:, 10:12], gn[:, 8:10], ALU.add).then_inc(gn_step, 1)
                dve.wait_ge(gn_step, 6 * b + 5)
                dve.tensor_scalar(gn[:, 12:14], gn[:, 10:12], 0.5, None, ALU.mult).then_inc(gn_step, 1)
                dve.wait_ge(gn_step, 6 * b + 6)
                dve.reciprocal(gn_scale[:, :], gn[:, 12:14]).then_inc(gn_dve, 1)
                dve.wait_ge(gn_dve, 5 * b + 4)
                dve.scalar_tensor_tensor(gn_bias[:, :], gn_scale[:, :], -1.0, group[:, 0], ALU.mult, ALU.mult).then_inc(gn_dve, 1)

                def add_scores(i, c, h):
                    n = 8 * (STEPS * b + 4 * i + c - 2) + h
                    dve.wait_ge(scores_ready, n + 1)
                    dve.tensor_tensor(scores[:, h, :], scores[:, h, :], psum[0:LP, 6 + h % 2, 0:2 * L],
                                      ALU.add).then_inc(scores_added, 1)

                def step1(i, c):
                    T, n = SETS * b + 4 * i + c, STEPS * b + 4 * i + c - 2
                    own = u1[:, 2, :, PE_CHUNKS:CHUNKS], conv1[:, 2, PE_CHUNKS:CHUNKS]

                    def add_due(k):
                        for h in range(HEADS):
                            if ADD_SLOTS[h] == k and not first(i, c, 3):
                                add_scores(*move(i, c, -1), h)

                    def tap(m, k, before):
                        if k == 1:
                            dve.wait_ge(tap0_done, 3 * n + m + 1)
                        u_in, acc = (u1[:, m], conv1[:, m]) if m < 2 else own
                        tap_sum(u_in, c, k, taps[:, m], acc, mac1, conv1_done, 21 * n + before)

                    def sets_there(k, m):
                        if k == 6 or k == 3 and first(i, c, 3):
                            dve.wait_ge(u1_evac, 6 * (T - 2 + k // 3) + 2 * m + 2)

                    for k in range(1, 9):
                        sets_there(k, 0)
                        tap(0, k, k - 1)
                        add_due(k)
                    for k in range(1, 9):
                        sets_there(k, 2)
                        tap(1, k, 7 + 2 * k - 3)
                        tap(2, k, 7 + 2 * k - 2)
                        add_due(9 + k)

                walk(dve, step1)
                for h in range(HEADS):
                    add_scores(STEPS // 4 - 1, 5, h)

                def small(ins, k):
                    ins.then_inc(soft_step, 1)
                    dve.wait_ge(soft_step, 7 * b + k)

                dve.wait_ge(soft_act, 2 * b + 1)
                small(dve.tensor_scalar(nrm[:, 1], nrm[:, 0], NORM_EPS, None, ALU.max), 1)
                small(dve.reciprocal(nrm[:, 2], nrm[:, 1]), 2)
                small(dve.tensor_tensor(nrm[:, 2], nrm[:, 2], sumsq[:, :, :], ALU.mult), 3)
                small(dve.tensor_tensor(nrm[:, 2], nrm[:, 2], nrm[:, 1], ALU.add), 4)
                small(dve.tensor_scalar(nrm[:, 2], nrm[:, 2], 0.5, NORM_EPS, ALU.mult, ALU.max), 5)
                dve.reciprocal(nrm[:, 3], nrm[:, 2]).then_inc(soft_dve, 1)
                dve.wait_ge(soft_dma, DMA * 3 * (b + 1))
                small(dve.tensor_tensor(row_scale[:, :, :], row_scale[:, :, :],
                                        temp[:, :].rearrange("p (h o) -> p h o", o=1).to_broadcast([LP, HEADS, 2]), ALU.mult), 6)
                for h in range(HEADS):
                    for g in range(2):
                        ins = dve.scalar_tensor_tensor(logits[:, h, g, :], scores[:, h, L * g:L * (g + 1)],
                                                       row_scale[:, h, g:g + 1], k_scale[:, h, :], ALU.mult, ALU.mult)
                ins.then_inc(soft_dve, 1)
                dve.wait_ge(soft_dve, 5 * b + 2)
                small(dve.tensor_reduce(soft[:, 0], logits[:, :, :, :], AX_X, ALU.max), 7)
                dve.tensor_scalar(soft[:, 1], soft[:, 0], -1.0, None, ALU.mult).then_inc(soft_dve, 1)
                dve.wait_ge(soft_act, 2 * b + 2)
                dve.reciprocal(soft[:, 3], soft[:, 2]).then_inc(soft_dve, 1)
                dve.wait_ge(soft_dve, 5 * b + 4)
                flat = logits[:, :, :, :].rearrange("p h g n -> p (h g) n")
                dve.tensor_tensor(flat, flat, soft[:, 3].rearrange("p h (g o) -> p (h g) o", o=1).to_broadcast(
                    [LP, HEADS * 2, L]), ALU.mult).then_inc(soft_dve, 1)

                def add_resid(i, c, g):
                    q, n = c % 2, STEPS * b + 4 * i + c - 2
                    if g == 0:
                        dve.wait_ge(resid_loaded[q], 3 * DMA * (STEPS // 2 * b + 2 * i + (c - 2) // 2 + 1))
                    dve.wait_ge(proj_ready, 6 * n + g + 1)
                    part = resid[:, q, 2 * g:2 * g + 2, :]
                    dve.tensor_tensor(part, part, psum[:, 6 + g % 2, :].rearrange("p (s w) -> p s w", s=2),
                                      ALU.add).then_inc(resid_done, 1)

                def step2(i, c):
                    T, n = SETS * b + 4 * i + c, STEPS * b + 4 * i + c - 2
                    q = c % 2
                    for m in range(2):
                        dve.wait_ge(v_tap0_done, 2 * n + m + 1)
                        for k in range(1, 9):
                            if k == 6 or k == 3 and first(i, c, 3):
                                dve.wait_ge(u2_evac, 6 * (T - 2 + k // 3) + (4, 6)[m])
                            tap_sum((u2_main, u2_rest)[m], c, k, taps[:, 3 + m], (v_main, v_rest)[m][:, q], mac2,
                                    conv2_done, 14 * n + 7 * m + k - 1)
                            if more and m == 0 and k in NEXT_AT:
                                chunk = NEXT_AT.index(k)
                                dve.wait_ge(gn_next_loaded[chunk], DMA * (n + 1))
                                gn_stats(gn_next_in[chunk], (NEXT_SLOTS * (4 * i + c - 2) + chunk) * (NEXT_CHUNK // BN))
                            for g in range(6):
                                if RESID_SLOTS[g] == 9 * m + k and not first(i, c, 4):
                                    add_resid(*move(i, c, -2), g)

                walk(dve, step2)
                for c in (4, 5):
                    for g in range(6):
                        add_resid(STEPS // 4 - 1, c, g)
                if more:
                    for q in range(2):
                        dve.wait_ge(out_stored[q], 3 * DMA * STEPS // 2 * (b + 1))

            batches(dve, batch)

        @block.gpsimd
        def _(pool):
            pool.memset(zeros[:, :], 0.0).then_inc(zeroed, 1)
            with pool.Fori(0, BATCH) as b:
                def step(i, c):
                    n = STEPS * b + 4 * i + c - 2
                    if first(i, c, 3):
                        pool.wait_ge(sums_zeroed, b + 1)
                    else:
                        pool.wait_ge(sq_added, n)
                    pool.wait_ge(squared, 3 * (n + 1))
                    pool.tensor_tensor(sumsq[:, :, :], sumsq[:, :, :], sq_step[:, c % 2], ALU.add).then_inc(sq_added, 1)

                walk(pool, step)


def kernel(x, L0_conv_qkv_w, L0_conv_dw_w, L0_conv_proj_w, L0_conv_temperature):
    import numpy as np
    import concourse.bacc as bacc
    from concourse.bass_utils import run_bass_kernel_spmd

    p = np.arange(P)
    ident = np.eye(P, dtype=np.float32)
    group_avg = np.where(p[:, None] // 4 == p[None, :] // 4, 0.25, 0.0).astype(np.float32)
    channel = np.stack([p, P + p % REST])
    per_group = C // GROUPS
    group_sel = np.where(p[:, None, None] // 4 == channel[None] // per_group, 0.25, 0.0).astype(np.float32)

    arrays = {
        "x_in": np.ascontiguousarray(x),
        "w_qkv_t": np.ascontiguousarray(np.asarray(L0_conv_qkv_w).T),
        "dw_in": np.ascontiguousarray(np.asarray(L0_conv_dw_w).reshape(3 * C, 9)),
        "proj_t": np.ascontiguousarray(np.asarray(L0_conv_proj_w).T),
        "temperature": np.ascontiguousarray(np.asarray(L0_conv_temperature).reshape(1, HEADS)),
        "ident_in": ident,
        "group_avg_in": group_avg,
        "group_sel_in": group_sel,
    }
    nc = bacc.Bacc("TRN2", target_bir_lowering=False, num_devices=1)
    args = [nc.dram_tensor(name, a.shape, mybir.dt.from_np(a.dtype), kind="ExternalInput").ap()
            for name, a in arrays.items()]
    out = nc.dram_tensor("out_dram", (BATCH, C, H, W), F32, kind="ExternalOutput").ap()
    conv_preact_kernel(nc, *args, out)
    r = run_bass_kernel_spmd(nc, [arrays], core_ids=[0])
    return r.results[0]["out_dram"]
```
